# Optimizing a Trainium2 kernel written in Bass

```python
import numpy as np
import jax
import jax.numpy as jnp

def _softmax(x, axis=-1):
    return jax.nn.softmax(x, axis=axis)

def _gelu(x):
    return jax.nn.gelu(x, approximate=True)

def _silu(x):
    return jax.nn.silu(x)

def _sigmoid(x):
    return jax.nn.sigmoid(x)

def _layernorm(x, axis=-1, eps=1e-05):
    m = jnp.mean(x, axis=axis, keepdims=True)
    v = jnp.var(x, axis=axis, keepdims=True)
    return (x - m) / jnp.sqrt(v + eps)

def _scatter_add(tgt, idx, src, axis=0):
    return tgt.at[idx].add(src)

def _segment_sum(src, seg, n):
    return jax.ops.segment_sum(src, seg, n)
kernel_name = 'mk_lm_tower_d2_tok_ids1024_r4_09c16f'

def setup_inputs(seed: int=0):
    np.random.seed(seed)
    _w = jnp.asarray

    def _rec_inputs():
        import jax
        import jax.numpy as jnp
        _rk = jax.random.key(seed)
        x = jax.random.randint(jax.random.fold_in(_rk, 1), (2, 2048), 0, 12564, jnp.int32)
        return x
    x = _rec_inputs()

    def _L0_tok_setup():
        import jax, jax.numpy as jnp
        import numpy as np
        VOCAB = 50257
        CUTOFFS = [0, 5000, 10000, VOCAB]
        DIV_VAL = 4
        BASE_DIM = 256
        PROJ_DIM = 256
        EMB_DIMS = [BASE_DIM // DIV_VAL ** i for i in range(3)]
        SCALE = PROJ_DIM ** 0.5
        key = jax.random.key(seed)
        ks = jax.random.split(key, 10)
        x = jax.random.randint(ks[0], (8, 1024), 0, VOCAB, dtype=jnp.int64)
        inp = {'x': x}
        for i in range(3):
            l, r = (CUTOFFS[i], CUTOFFS[i + 1])
            n_rows = r - l + (1 if i == 2 else 0)
            d = EMB_DIMS[i]
            inp[f'emb{i}'] = jax.random.normal(ks[1 + i], (n_rows, d), dtype=jnp.float32)
            inp[f'w{i}'] = jax.random.normal(ks[4 + i], (PROJ_DIM, d), dtype=jnp.float32) / np.sqrt(d)
            inp[f'b{i}'] = jax.random.normal(ks[7 + i], (PROJ_DIM,), dtype=jnp.float32) * 0.01
        return inp
    _L0_tok_all = _L0_tok_setup()
    _L0_tok_in = {k: v for k, v in _L0_tok_all.items() if k in ('emb0', 'emb1', 'emb2', 'w0', 'b0', 'w1', 'b1', 'w2', 'b2')}
    del _L0_tok_all

    def _L0_attn_setup():
        import jax, jax.numpy as jnp
        import numpy as np
        DIM = 256
        HEADS = 16
        DIM_HEAD = DIM // HEADS
        LATENT = DIM // 4
        SCALE = DIM_HEAD ** (-0.5)
        key = jax.random.key(seed)
        ks = jax.random.split(key, 8)
        B, S = (2, 512)
        init = lambda k, shape, fan_in: jax.random.normal(k, shape, jnp.float32) * fan_in ** (-0.5)
        return {'x': jax.random.normal(ks[0], (B, S, DIM), jnp.float32), 'Wq': init(ks[1], (DIM, DIM), DIM), 'bq': jnp.zeros((DIM,), jnp.float32), 'Wl': init(ks[2], (DIM, LATENT), DIM), 'bl': jnp.zeros((LATENT,), jnp.float32), 'Wk': init(ks[3], (LATENT, DIM), LATENT), 'bk': jnp.zeros((DIM,), jnp.float32), 'Wv': init(ks[4], (LATENT, DIM), LATENT), 'bv': jnp.zeros((DIM,), jnp.float32), 'Wo': init(ks[5], (DIM, DIM), DIM), 'bo': jnp.zeros((DIM,), jnp.float32)}
    _L0_attn_all = _L0_attn_setup()
    _L0_attn_in = {k: v for k, v in _L0_attn_all.items() if k in ('Wq', 'bq', 'Wl', 'bl', 'Wk', 'bk', 'Wv', 'bv', 'Wo', 'bo')}
    del _L0_attn_all

    def _L0_ffn_setup():
        import jax, jax.numpy as jnp
        import numpy as np
        from jax import lax
        B, S, D = (4, 512, 256)
        E = 8
        K = 2
        F = 816
        NORM_TOPK = True
        key = jax.random.key(seed)
        ks = jax.random.split(key, 8)
        sd = 0.02
        return {'x': jax.random.normal(ks[0], (B, S, D), jnp.float32), 'gate_w': jax.random.normal(ks[1], (E, D), jnp.float32) * sd, 'gate_b': jnp.zeros((E,), jnp.float32), 'up_w': jax.random.normal(ks[2], (E, F, D), jnp.float32) * sd, 'up_b': jnp.zeros((E, F), jnp.float32), 'gp_w': jax.random.normal(ks[3], (E, F, D), jnp.float32) * sd, 'gp_b': jnp.zeros((E, F), jnp.float32), 'down_w': jax.random.normal(ks[4], (E, D, F), jnp.float32) * sd, 'down_b': jnp.zeros((E, D), jnp.float32)}
    _L0_ffn_all = _L0_ffn_setup()
    _L0_ffn_in = {k: v for k, v in _L0_ffn_all.items() if k in ('gate_w', 'gate_b', 'up_w', 'up_b', 'gp_w', 'gp_b', 'down_w', 'down_b')}
    del _L0_ffn_all

    def _L1_attn_setup():
        import jax, jax.numpy as jnp
        import numpy as np
        DIM = 256
        NUM_HEADS = 16
        HEAD_DIM = DIM // NUM_HEADS
        SCALE = HEAD_DIM ** (-0.5)

        def alibi_slopes(num_heads):
            x = (2 ** 8) ** (1.0 / num_heads)
            return jnp.array([1.0 / x ** (i + 1) for i in range(num_heads)], dtype=jnp.float32)
        key = jax.random.key(seed)
        ks = jax.random.split(key, 6)
        B, N = (2, 512)
        x = jax.random.normal(ks[0], (B, N, DIM), dtype=jnp.float32)
        s = DIM ** (-0.5)
        Wq = jax.random.normal(ks[1], (DIM, DIM), dtype=jnp.float32) * s
        Wk = jax.random.normal(ks[2], (DIM, DIM), dtype=jnp.float32) * s
        Wv = jax.random.normal(ks[3], (DIM, DIM), dtype=jnp.float32) * s
        Wp = jax.random.normal(ks[4], (DIM, DIM), dtype=jnp.float32) * s
        bp = jnp.zeros((DIM,), dtype=jnp.float32)
        return {'x': x, 'Wq': Wq, 'Wk': Wk, 'Wv': Wv, 'Wp': Wp, 'bp': bp}
    _L1_attn_all = _L1_attn_setup()
    _L1_attn_in = {k: v for k, v in _L1_attn_all.items() if k in ('Wq', 'Wk', 'Wv', 'Wp', 'bp')}
    del _L1_attn_all

    def _L1_ffn_setup():
        import jax, jax.numpy as jnp
        import numpy as np
        BLOCK = 16
        _GRID = jnp.array([0.0, 0.5, 1.0, 1.5, 2.0, 3.0, 4.0, 6.0], dtype=jnp.float32)
        _MID = jnp.array([0.25, 0.75, 1.25, 1.75, 2.5, 3.5, 5.0], dtype=jnp.float32)

        def fp4_quant_dequant(x):
            shape = x.shape
            xb = x.reshape(shape[:-1] + (shape[-1] // BLOCK, BLOCK))
            scale = jnp.max(jnp.abs(xb), axis=-1, keepdims=True) / 6.0
            scale = jnp.maximum(scale, jnp.float32(1e-12))
            xn = xb / scale
            idx = jnp.searchsorted(_MID, jnp.abs(xn))
            q = _GRID[idx] * jnp.sign(xn) * scale
            return q.reshape(shape)

        def fp4_linear(x, w):
            xq = fp4_quant_dequant(x)
            wq = fp4_quant_dequant(w)
            return jnp.einsum('bsk,nk->bsn', xq, wq)
        key = jax.random.key(seed)
        k1, k2, k3, k4 = jax.random.split(key, 4)
        H, I = (256, 704)
        x = jax.random.normal(k1, (4, 1024, H), dtype=jnp.float32)
        w_gate = jax.random.normal(k2, (I, H), dtype=jnp.float32) * 0.02
        w_up = jax.random.normal(k3, (I, H), dtype=jnp.float32) * 0.02
        w_down = jax.random.normal(k4, (H, I), dtype=jnp.float32) * 0.02
        return {'x': x, 'w_gate': w_gate, 'w_up': w_up, 'w_down': w_down}
    _L1_ffn_all = _L1_ffn_setup()
    _L1_ffn_in = {k: v for k, v in _L1_ffn_all.items() if k in ('w_gate', 'w_up', 'w_down')}
    del _L1_ffn_all
    return {'x': x, 'L0_tok_emb0': _L0_tok_in['emb0'], 'L0_tok_emb1': _L0_tok_in['emb1'], 'L0_tok_emb2': _L0_tok_in['emb2'], 'L0_tok_w0': _L0_tok_in['w0'], 'L0_tok_b0': _L0_tok_in['b0'], 'L0_tok_w1': _L0_tok_in['w1'], 'L0_tok_b1': _L0_tok_in['b1'], 'L0_tok_w2': _L0_tok_in['w2'], 'L0_tok_b2': _L0_tok_in['b2'], 'L0_attn_Wq': _L0_attn_in['Wq'], 'L0_attn_bq': _L0_attn_in['bq'], 'L0_attn_Wl': _L0_attn_in['Wl'], 'L0_attn_bl': _L0_attn_in['bl'], 'L0_attn_Wk': _L0_attn_in['Wk'], 'L0_attn_bk': _L0_attn_in['bk'], 'L0_attn_Wv': _L0_attn_in['Wv'], 'L0_attn_bv': _L0_attn_in['bv'], 'L0_attn_Wo': _L0_attn_in['Wo'], 'L0_attn_bo': _L0_attn_in['bo'], 'L0_ffn_gate_w': _L0_ffn_in['gate_w'], 'L0_ffn_gate_b': _L0_ffn_in['gate_b'], 'L0_ffn_up_w': _L0_ffn_in['up_w'], 'L0_ffn_up_b': _L0_ffn_in['up_b'], 'L0_ffn_gp_w': _L0_ffn_in['gp_w'], 'L0_ffn_gp_b': _L0_ffn_in['gp_b'], 'L0_ffn_down_w': _L0_ffn_in['down_w'], 'L0_ffn_down_b': _L0_ffn_in['down_b'], 'L1_attn_Wq': _L1_attn_in['Wq'], 'L1_attn_Wk': _L1_attn_in['Wk'], 'L1_attn_Wv': _L1_attn_in['Wv'], 'L1_attn_Wp': _L1_attn_in['Wp'], 'L1_attn_bp': _L1_attn_in['bp'], 'L1_ffn_w_gate': _L1_ffn_in['w_gate'], 'L1_ffn_w_up': _L1_ffn_in['w_up'], 'L1_ffn_w_down': _L1_ffn_in['w_down']}

def reference(x, L0_tok_emb0, L0_tok_emb1, L0_tok_emb2, L0_tok_w0, L0_tok_b0, L0_tok_w1, L0_tok_b1, L0_tok_w2, L0_tok_b2, L0_attn_Wq, L0_attn_bq, L0_attn_Wl, L0_attn_bl, L0_attn_Wk, L0_attn_bk, L0_attn_Wv, L0_attn_bv, L0_attn_Wo, L0_attn_bo, L0_ffn_gate_w, L0_ffn_gate_b, L0_ffn_up_w, L0_ffn_up_b, L0_ffn_gp_w, L0_ffn_gp_b, L0_ffn_down_w, L0_ffn_down_b, L1_attn_Wq, L1_attn_Wk, L1_attn_Wv, L1_attn_Wp, L1_attn_bp, L1_ffn_w_gate, L1_ffn_w_up, L1_ffn_w_down):
    import jax
    import jax.numpy as jnp

    def _L0_tok_ref(x, emb0, emb1, emb2, w0, b0, w1, b1, w2, b2):
        import jax, jax.numpy as jnp
        import numpy as np
        VOCAB = 50257
        CUTOFFS = [0, 5000, 10000, VOCAB]
        DIV_VAL = 4
        BASE_DIM = 256
        PROJ_DIM = 256
        EMB_DIMS = [BASE_DIM // DIV_VAL ** i for i in range(3)]
        SCALE = PROJ_DIM ** 0.5
        embs = [emb0, emb1, emb2]
        ws = [w0, w1, w2]
        bs = [b0, b1, b2]
        flat_x = x.reshape(-1)
        out = jnp.zeros((flat_x.shape[0], PROJ_DIM), dtype=jnp.float32)
        for i in range(3):
            l, r = (CUTOFFS[i], CUTOFFS[i + 1])
            if i == 2:
                r += 1
            mask = (flat_x >= l) & (flat_x < r)
            idx = jnp.clip(flat_x - l, 0, embs[i].shape[0] - 1)
            e = embs[i][idx]
            p = jnp.einsum('nd,pd->np', e, ws[i]) + bs[i]
            out = out + jnp.where(mask[:, None], p, 0.0)
        out = out.reshape(*x.shape, PROJ_DIM) * SCALE
        return out

    def _L0_attn_ref(x, Wq, bq, Wl, bl, Wk, bk, Wv, bv, Wo, bo):
        import jax, jax.numpy as jnp
        import numpy as np
        DIM = 256
        HEADS = 16
        DIM_HEAD = DIM // HEADS
        LATENT = DIM // 4
        SCALE = DIM_HEAD ** (-0.5)
        B, S, D = x.shape
        H, Dh = (HEADS, DIM_HEAD)
        q = (x @ Wq + bq).reshape(B, S, H, Dh)
        latent = x @ Wl + bl
        k = (latent @ Wk + bk).reshape(B, S, H, Dh)
        v = (latent @ Wv + bv).reshape(B, S, H, Dh)
        scores = jnp.einsum('bihd,bjhd->bhij', q, k) * SCALE
        attn = jax.nn.softmax(scores, axis=-1)
        out = jnp.einsum('bhij,bjhd->bihd', attn, v).reshape(B, S, D)
        out = out @ Wo + bo
        return out

    def _L0_ffn_ref(x, gate_w, gate_b, up_w, up_b, gp_w, gp_b, down_w, down_b):
        import jax, jax.numpy as jnp
        import numpy as np
        from jax import lax
        B, S, D = (4, 512, 256)
        E = 8
        K = 2
        F = 816
        NORM_TOPK = True
        bs, slen, dim = x.shape
        xf = x.reshape(-1, dim)
        N = xf.shape[0]
        scores = jax.nn.softmax(xf @ gate_w.T + gate_b, axis=-1)
        top_w, top_idx = lax.top_k(scores, K)
        if NORM_TOPK:
            top_w = top_w / (top_w.sum(-1, keepdims=True) + 1e-20)
        comb = jnp.zeros((N, E), xf.dtype).at[jnp.arange(N)[:, None], top_idx].add(top_w)

        def step(acc, p):
            uw, ub, gw, gb, dw, db, w = p
            h = jax.nn.silu((xf @ gw.T + gb) * (xf @ uw.T + ub))
            return (acc + w[:, None] * (h @ dw.T + db), None)
        y0 = jnp.zeros_like(xf)
        y, _ = lax.scan(step, y0, (up_w, up_b, gp_w, gp_b, down_w, down_b, comb.T))
        return y.reshape(bs, slen, dim)

    def _L1_attn_ref(x, Wq, Wk, Wv, Wp, bp):
        import jax, jax.numpy as jnp
        import numpy as np
        DIM = 256
        NUM_HEADS = 16
        HEAD_DIM = DIM // NUM_HEADS
        SCALE = HEAD_DIM ** (-0.5)

        def alibi_slopes(num_heads):
            x = (2 ** 8) ** (1.0 / num_heads)
            return jnp.array([1.0 / x ** (i + 1) for i in range(num_heads)], dtype=jnp.float32)
        B, N, C = x.shape
        H, D = (NUM_HEADS, HEAD_DIM)
        q = (x @ Wq.T).reshape(B, N, H, D).transpose(0, 2, 1, 3)
        k = (x @ Wk.T).reshape(B, N, H, D).transpose(0, 2, 1, 3)
        v = (x @ Wv.T).reshape(B, N, H, D).transpose(0, 2, 1, 3)
        rel = (jnp.arange(N)[None, :] - jnp.arange(N)[:, None]).astype(jnp.float32)
        bias = alibi_slopes(H)[:, None, None] * rel
        score = jnp.einsum('bhnd,bhmd->bhnm', q, k) / SCALE + bias[None]
        attn = jax.nn.softmax(score, axis=-1)
        out = jnp.einsum('bhnm,bhmd->bhnd', attn, v)
        out = out.transpose(0, 2, 1, 3).reshape(B, N, C)
        return out @ Wp.T + bp

    def _L1_ffn_ref(x, w_gate, w_up, w_down):
        import jax, jax.numpy as jnp
        import numpy as np
        BLOCK = 16
        _GRID = jnp.array([0.0, 0.5, 1.0, 1.5, 2.0, 3.0, 4.0, 6.0], dtype=jnp.float32)
        _MID = jnp.array([0.25, 0.75, 1.25, 1.75, 2.5, 3.5, 5.0], dtype=jnp.float32)

        def fp4_quant_dequant(x):
            shape = x.shape
            xb = x.reshape(shape[:-1] + (shape[-1] // BLOCK, BLOCK))
            scale = jnp.max(jnp.abs(xb), axis=-1, keepdims=True) / 6.0
            scale = jnp.maximum(scale, jnp.float32(1e-12))
            xn = xb / scale
            idx = jnp.searchsorted(_MID, jnp.abs(xn))
            q = _GRID[idx] * jnp.sign(xn) * scale
            return q.reshape(shape)

        def fp4_linear(x, w):
            xq = fp4_quant_dequant(x)
            wq = fp4_quant_dequant(w)
            return jnp.einsum('bsk,nk->bsn', xq, wq)
        gate = fp4_linear(x, w_gate)
        y = fp4_linear(x, w_up)
        h = jax.nn.silu(gate) * y
        return fp4_linear(h, w_down)
    h = _L0_tok_ref(x, L0_tok_emb0, L0_tok_emb1, L0_tok_emb2, L0_tok_w0, L0_tok_b0, L0_tok_w1, L0_tok_b1, L0_tok_w2, L0_tok_b2)
    h = h + _L0_attn_ref(_layernorm(h, axis=-1), L0_attn_Wq, L0_attn_bq, L0_attn_Wl, L0_attn_bl, L0_attn_Wk, L0_attn_bk, L0_attn_Wv, L0_attn_bv, L0_attn_Wo, L0_attn_bo)
    h = h + _L0_ffn_ref(_layernorm(h, axis=-1), L0_ffn_gate_w, L0_ffn_gate_b, L0_ffn_up_w, L0_ffn_up_b, L0_ffn_gp_w, L0_ffn_gp_b, L0_ffn_down_w, L0_ffn_down_b)
    h = h + _L1_attn_ref(_layernorm(h, axis=-1), L1_attn_Wq, L1_attn_Wk, L1_attn_Wv, L1_attn_Wp, L1_attn_bp)
    h = h + _L1_ffn_ref(_layernorm(h, axis=-1), L1_ffn_w_gate, L1_ffn_w_up, L1_ffn_w_down)
    return h

_drawn_inputs = setup_inputs


def setup_inputs(seed=0):
    import zlib

    import numpy as np

    out = dict(_drawn_inputs(seed))
    spreads = {'L0_attn_bq': (0.0, 0.8),
     'L0_attn_bl': (0.0, 0.8),
     'L0_attn_bk': (0.0, 2.0),
     'L0_attn_bv': (0.0, 2.0),
     'L0_attn_bo': (0.0, 2.0),
     'L0_ffn_gate_b': (0.0, 0.8),
     'L0_ffn_up_b': (0.0, 0.8),
     'L0_ffn_gp_b': (0.0, 0.8),
     'L0_ffn_down_b': (0.0, 2.0),
     'L1_attn_bp': (0.0, 2.0)}
    factors = {'L0_tok_b0': 8.0,
     'L0_tok_b1': 8.0,
     'L0_tok_b2': 8.0,
     'L0_attn_Wq': 5.314,
     'L0_attn_Wl': 7.822,
     'L0_attn_Wk': 5.29,
     'L0_attn_Wv': 4.549,
     'L0_attn_Wo': 3.938,
     'L0_ffn_gate_w': 8.0,
     'L0_ffn_up_w': 8.0,
     'L0_ffn_gp_w': 8.0,
     'L0_ffn_down_w': 8.0,
     'L1_ffn_w_gate': 8.0,
     'L1_ffn_w_up': 8.0,
     'L1_ffn_w_down': 8.0,
     'L1_attn_Wq': 5.264,
     'L1_attn_Wk': 5.243,
     'L1_attn_Wv': 5.202,
     'L1_attn_Wp': 5.2}
    for name, (base, spread) in spreads.items():
        noise = np.random.default_rng([zlib.crc32(name.encode()), seed]).standard_normal(out[name].shape)
        drawn = base * np.exp(spread * noise) if base else spread * noise
        out[name] = jnp.asarray(drawn.astype(out[name].dtype))
    for name, factor in factors.items():
        out[name] = (out[name] * factor).astype(out[name].dtype)
    return out
```

```python
from contextlib import ExitStack

import numpy as np

import concourse.bass as bass
from concourse import mybir

F32 = mybir.dt.float32
BF16 = mybir.dt.bfloat16
I32 = mybir.dt.int32
ALU = mybir.AluOpType
ACT = mybir.ActivationFunctionType
AX = mybir.AxisListType

BATCH, SEQ, DIM = 2, 2048, 256
HEADS, HEAD_DIM = 16, 16
PAIRS = BATCH * HEADS
TOKENS = BATCH * SEQ
TILES = TOKENS // 128
HALVES = DIM // 128
CHUNK = 4
EPS = 1e-5
LATENT = DIM // 4

CUTOFFS = (0, 5000, 10000, 50258)
EMB_DIMS = (256, 64, 16)
CAT = sum(EMB_DIMS) + 3

EXPERTS, FFN = 8, 816
FT = -(-FFN // 128)
FREST = FFN - (FT - 1) * 128
BLOCK = 256
BLOCKS = -(-(2 * TOKENS + EXPERTS * (BLOCK - 1)) // BLOCK)
BLOCKS += BLOCKS % 2
SUBS = BLOCK // 128
UP, GATE, DOWN, UPB, GATEB = 0, 2 * FFN, 4 * FFN, 4 * FFN + FT * DIM, 4 * FFN + FT * DIM + FT
EROW = GATEB + FT

INNER = 704
QUANT = 16
IT = -(-INNER // 128)
IREST = INNER - (IT - 1) * 128


class Chain:

    def __init__(self, eng, sem):
        self.eng, self.sem, self.n = eng, sem, 0

    def step(self, ins):
        ins.then_inc(self.sem, 1)
        self.n += 1
        self.eng.wait_ge(self.sem, self.n)


class Head:

    def __init__(self, turn, c):
        self.turn, self.c = turn, c
        self.n = turn * 4 + c
        self.slot = c % 4
        self.fills = turn + (c // 4 + 1)
        self.first = isinstance(turn, int) and c == 0

    def ahead(self, k):
        return Head(self.turn, self.c + k)

    def at_least(self, k):
        return not isinstance(self.turn, int) or self.c >= k


def attention_core(nc, parts_q, parts_k, values, attended, bias_rows, scale, heads, tag):
    with ExitStack() as ctx:
        sb, pm, sem = alloc(nc, ctx, tag)

        KT = SEQ // 128
        QB = SEQ // 512
        NB = QB * KT
        NA = KT * SEQ // 1024
        GROUP = 4
        NG = NB // GROUP
        AHEAD = 4
        KD = 6 * HEAD_DIM
        KS = KD + (6 if bias_rows else 0)
        KM = KS + 3
        LOADS = 6 + (2 if bias_rows else 0)

        q_rows = [sb(f"q_rows{s}", [128, SEQ], BF16) for s in range(4)]
        k_rows = [sb(f"k_rows{s}", [128, SEQ], BF16) for s in range(4)]
        v_ones = [sb(f"v_ones{s}", [128, KT, 32], F32) for s in range(4)]
        probs = [sb(f"probs{s}", [128, 512], F32) for s in range(8)]
        out_t = sb("out_t", [128, SEQ], F32)
        fold = sb("fold", [128, 17], F32)
        fold_i = sb("fold_i", [128, 17], F32)
        ident = sb("ident", [128, 128], BF16)
        half_max = sb("half_max", [128, 2, KT, 2], F32)
        row_max = sb("row_max", [128, KT], F32)
        rest = sb("rest", [128, KT], F32)
        rest2 = sb("rest2", [128, KT], F32)
        max_parts = sb("max_parts", [128, 128], BF16)
        max_rows = [sb(f"max_rows{s}", [3 * KT, 128], BF16) for s in range(2)]
        inv = sb("inv", [128, KT], F32)

        ps_max = [pm(f"ps_max{s}", [128, 1024], F32) for s in range(2)]
        ps_s = [pm(f"ps_s{s}", [128, 512], F32) for s in range(2)]
        ps_o = pm("ps_o", [128, 512], F32)
        ps_x = pm("ps_x", [128, 512], F32)
        ps_maxt = ps_x[:, 448:512].bitcast(BF16)

        const_ready = sem("const_ready")
        ones_ready = sem("ones_ready")
        loaded = [sem(f"loaded{s}") for s in range(4)]
        max_in_place = [sem(f"max_in_place{s}") for s in range(4)]
        v_filled = sem("v_filled")
        v_ready = sem("v_ready")
        half_scored = sem("half_scored")
        half_reduced = sem("half_reduced")
        split_step = sem("split_step")
        max_turned = sem("max_turned")
        max_copied = sem("max_copied")
        scored = sem("scored")
        exp_done = sem("exp_done")
        pv_done = sem("pv_done")
        out_copied = sem("out_copied")
        folded = sem("folded")
        inverted = sem("inverted")
        normed = sem("normed")
        fold_step = sem("fold_step")
        SPLITS = 6

        block = ctx.enter_context(nc.Block())

        LOOPS = (heads - 4) // 4
        assert LOOPS * 4 == heads - 4

        def every_head(eng, step):
            step(Head(0, 0), 3)
            with eng.Fori(0, LOOPS) as i:
                for u in range(1, 5):
                    step(Head(i, u), 3)
            for c in range(heads - 3, heads):
                step(Head(0, c), heads - 1 - c)

        @block.sync
        def _(sp):
            def load(h):
                q, k = q_rows[h.slot], k_rows[h.slot]
                for part, copies, at in ((0, 3, 0), (1, 2, 3), (2, 1, 5)):
                    a, b = at * HEAD_DIM, (at + copies) * HEAD_DIM
                    sp.dma_start(q[a:b, :], parts_q[part, bass.ds(h.n, 1), :, :].to_broadcast(
                        [copies, HEAD_DIM, SEQ])).then_inc(loaded[h.slot], 16)
                    sp.dma_start(k[a:b, :], parts_k[0:copies, bass.ds(h.n, 1), :, :].rearrange("c a d n -> c (a d) n")
                                 ).then_inc(loaded[h.slot], 16)
                if bias_rows:
                    for rows, table in ((q, bias_rows[0]), (k, bias_rows[1])):
                        sp.dma_start(rows[KD:KS, :], table[bass.ds(h.n, 1), :, :].rearrange("a d n -> (a d) n")
                                     ).then_inc(loaded[h.slot], 16)

            sp.wait_ge(ones_ready, 4)
            for s in range(3):
                load(Head(0, s))

            def place_max(h):
                sp.wait_ge(max_copied, h.n + 1)
                for part in range(3):
                    sp.dma_start(q_rows[h.slot][KS + part:KS + part + 1, :].rearrange("a (t n) -> a t n", n=128),
                                 max_rows[h.slot % 2][part * KT:(part + 1) * KT, :]).then_inc(max_in_place[h.slot], 16)

            def step(h, after):
                place_max(h)
                if after >= 3:
                    sp.wait_ge(scored, h.n * NB)
                    load(h.ahead(3))

            every_head(sp, step)

        @block.gpsimd
        def _(pool):
            nc.gpsimd.iota(fold_i[:], pattern=[[-1, 17]], base=128, channel_multiplier=1,
                           allow_small_or_imprecise_dtypes=True).then_inc(const_ready, 1)
            nc.gpsimd.memset(ident[:], 0.0).then_inc(const_ready, 1)
            pool.wait_ge(const_ready, 2)
            nc.gpsimd.affine_select(out=ident[:], in_=ident[:], compare_op=ALU.not_equal, fill=1.0, base=0,
                                    pattern=[[-1, 128]], channel_multiplier=1).then_inc(const_ready, 1)
            pool.wait_ge(v_filled, 8)

            def fetch_v(h):
                nc.gpsimd.tensor_copy(v_ones[h.slot][:, :, 0:HEAD_DIM],
                                      values[:, bass.ds(h.n, 1), :, :].rearrange("p a t d -> p (a t) d")).then_inc(v_ready, 1)

            for s in range(3):
                fetch_v(Head(0, s))

            def step(h, after):
                if after >= 3:
                    pool.wait_ge(pv_done, h.n * NG + 1)
                    fetch_v(h.ahead(3))

            every_head(pool, step)

        def half_rows_of_step(after):
            out = []
            for k in range(NA):
                ahead, n = (1, k + AHEAD) if k + AHEAD < NA else (2, k + AHEAD - NA)
                out.append((ahead, n) if ahead <= after else None)
            return out

        @block.tensor
        def _(pe):
            def score_half(h, n):
                if n == 0:
                    pe.wait_ge(loaded[h.slot], 16 * LOADS * h.fills)
                a = h.n * NA + n
                if h.at_least(1) or n >= 2:
                    pe.wait_ge(half_reduced, a - 1)
                q = q_rows[h.slot][0:KS, (n // 2) * 128:(n // 2 + 1) * 128]
                for c in range(2):
                    k0 = (n % 2) * 1024 + c * 512
                    m = nc.tensor.matmul(ps_max[n % 2][:, c * 512:(c + 1) * 512], q, k_rows[h.slot][0:KS, k0:k0 + 512],
                                         start=True, stop=True)
                m.then_inc(half_scored, 1)

            def turn_max(h):
                pe.wait_ge(split_step, SPLITS * (h.n + 1))
                if h.at_least(2):
                    pe.wait_ge(normed, h.n - 1)
                nc.tensor.transpose(ps_maxt[:, 0:128], max_parts[:],
                                    ident[:]).then_inc(max_turned, 1)

            def score(h, n):
                if n == 0:
                    pe.wait_ge(max_in_place[h.slot], 48 * h.fills)
                pe.wait_ge(exp_done, h.n * NB + n)
                qb, kt = n // KT, n % KT
                nc.tensor.matmul(ps_s[n % 2][:], k_rows[h.slot][0:KM, kt * 128:(kt + 1) * 128],
                                 q_rows[h.slot][0:KM, qb * 512:(qb + 1) * 512], start=True, stop=True).then_inc(scored, 1)

            def times_v(h, j):
                per = KT // GROUP
                if j == 0:
                    pe.wait_ge(v_ready, h.n + 1)
                if j % per == 0:
                    pe.wait_ge(out_copied, h.n * QB + j // per)
                pe.wait_ge(exp_done, h.n * NB + (j + 1) * GROUP + 1)
                for c in range(GROUP):
                    kt = (j % per) * GROUP + c
                    m = nc.tensor.matmul(ps_o[32 * c:32 * c + 32, :], v_ones[h.slot][:, kt, :],
                                         probs[(j % 2) * GROUP + c][:], start=(j % per == 0), stop=(j % per == per - 1))
                m.then_inc(pv_done, 1)

            def fold_out(h, after):
                pe.wait_ge(out_copied, (h.n + 1) * QB)
                pe.wait_ge(normed, h.n)
                pe.wait_ge(max_copied, h.n + 1 + (1 if after else 0))
                for t in range(KT):
                    m = nc.tensor.matmul(ps_x[:, t * 17:(t + 1) * 17], out_t[:, t * 128:(t + 1) * 128], fold[:],
                                         start=True, stop=True)
                m.then_inc(folded, 1)

            nc.tensor.nop().then_inc(pv_done, 1)
            pe.wait_ge(const_ready, 4)
            pe.wait_ge(ones_ready, 4)
            for n in range(NA):
                score_half(Head(0, 0), n)
            for n in range(AHEAD):
                score_half(Head(0, 1), n)
            turn_max(Head(0, 0))

            def step(h, after):
                halves = half_rows_of_step(after)
                turn_at = 2 * (NA - AHEAD) + 3
                for n in range(NB):
                    score(h, n)
                    if n == 9 and not h.first:
                        fold_out(h.ahead(-1), True)
                    if n % 2 == 1 and halves[n // 2]:
                        ahead, k = halves[n // 2]
                        score_half(h.ahead(ahead), k)
                    if n % 4 == 3 and n > 4:
                        times_v(h, n // 4 - 1)
                    if n == turn_at and after:
                        turn_max(h.ahead(1))
                times_v(h, NG - 1)

            every_head(pe, step)
            fold_out(Head(0, heads - 1), False)

        @block.scalar
        def _(act):
            def exps(h, n):
                act.wait_ge(scored, h.n * NB + n + 1)
                if n % GROUP == 0:
                    act.wait_ge(pv_done, h.n * NG + n // GROUP)
                nc.scalar.activation(probs[n % 8][:], ps_s[n % 2][:], ACT.Exp, scale=scale).then_inc(exp_done, 1)

            def copy_out(h, qb):
                act.wait_ge(pv_done, h.n * NG + (qb + 1) * (NG // QB) + 1)
                if qb == 0:
                    act.wait_ge(folded, h.n)
                nc.scalar.copy(out_t[:, qb * 512:(qb + 1) * 512], ps_o[:]).then_inc(out_copied, 1)

            def copy_max(h):
                act.wait_ge(max_turned, h.n + 1)
                if h.at_least(2):
                    act.wait_ge(max_in_place[h.ahead(-2).slot], 48 * h.ahead(-2).fills)
                nc.scalar.copy(max_rows[h.slot % 2][:], ps_maxt[0:3 * KT, 0:128]).then_inc(max_copied, 1)

            nc.scalar.nop().then_inc(exp_done, 1)
            copy_max(Head(0, 0))

            def step(h, after):
                for n in range(NB):
                    exps(h, n)
                    if n == 5 and not h.first:
                        copy_out(h.ahead(-1), QB - 1)
                    if n % KT == 5 and n > KT:
                        copy_out(h, n // KT - 1)
                    if n == 2 * (NA - AHEAD) + 5 and after:
                        copy_max(h.ahead(1))

            every_head(act, step)
            copy_out(Head(0, heads - 1), QB - 1)

        @block.vector
        def _(dve):
            def reduce_half(h, n):
                dve.wait_ge(half_scored, h.n * NA + n + 1)
                nc.vector.tensor_reduce(half_max[:, h.slot % 2, n // 2, n % 2:n % 2 + 1], ps_max[n % 2][:], AX.X, ALU.max
                                        ).then_inc(half_reduced, 1)

            def split_max(h):
                dve.wait_ge(half_reduced, (h.n + 1) * NA)
                if h.at_least(1):
                    dve.wait_ge(max_turned, h.n)
                hm = half_max[:, h.slot % 2, :, :]
                ops = [
                    lambda: nc.vector.tensor_reduce(row_max[:], hm, AX.X, ALU.max, negate=True),
                    lambda: nc.vector.tensor_copy(max_parts[:, 0 * KT:1 * KT], row_max[:]),
                    lambda: nc.vector.tensor_tensor(rest[:], row_max[:], max_parts[:, 0 * KT:1 * KT], ALU.subtract),
                    lambda: nc.vector.tensor_copy(max_parts[:, 1 * KT:2 * KT], rest[:]),
                    lambda: nc.vector.tensor_tensor(rest2[:], rest[:], max_parts[:, 1 * KT:2 * KT], ALU.subtract),
                    lambda: nc.vector.tensor_copy(max_parts[:, 2 * KT:3 * KT], rest2[:]),
                ]
                for n, op in enumerate(ops):
                    if n:
                        dve.wait_ge(split_step, h.n * SPLITS + n)
                    op().then_inc(split_step, 1)

            def norm(h):
                dve.wait_ge(folded, h.n + 1)
                turned = ps_x[:, 0:17 * KT].rearrange("p (t d) -> p t d", d=17)
                nc.vector.reciprocal(inv[:], turned[:, :, 16]).then_inc(inverted, 1)
                dve.wait_ge(inverted, h.n + 1)
                nc.vector.tensor_tensor(attended[:, bass.ds(h.n, 1), :, :].rearrange("p a t d -> p (a t) d"),
                                        turned[:, :, 0:HEAD_DIM], inv[:].unsqueeze(2).to_broadcast([128, KT, HEAD_DIM]),
                                        ALU.mult).then_inc(normed, 1)

            nc.vector.memset(max_parts[:], 0.0).then_inc(fold_step, 1)
            for s in range(4):
                nc.vector.memset(k_rows[s][96:128, :], 1.0).then_inc(ones_ready, 1)
            for s in range(4):
                nc.vector.memset(v_ones[s][:, :, 16:17], 1.0).then_inc(v_filled, 1)
                nc.vector.memset(v_ones[s][:, :, 17:32], 0.0).then_inc(v_filled, 1)
            dve.wait_ge(const_ready, 3)
            nc.vector.tensor_scalar(fold[:], fold_i[:], 128.0, None, ALU.is_equal).then_inc(fold_step, 1)
            for k in range(1, 4):
                dve.wait_ge(fold_step, k + 1)
                nc.vector.scalar_tensor_tensor(fold[:], fold_i[:], 128.0 + 32 * k, fold[:], ALU.is_equal, ALU.add
                                               ).then_inc(const_ready if k == 3 else fold_step, 1)
            for n in range(NA):
                reduce_half(Head(0, 0), n)
            split_max(Head(0, 0))
            for n in range(AHEAD):
                reduce_half(Head(0, 1), n)

            def step(h, after):
                for k, half in enumerate(half_rows_of_step(after)):
                    if half:
                        ahead, n = half
                        reduce_half(h.ahead(ahead), n)
                    if k == NA - AHEAD - 1 and after:
                        split_max(h.ahead(1))
                    if k == 9 and not h.first:
                        norm(h.ahead(-1))

            every_head(dve, step)
            norm(Head(0, heads - 1))


def alloc(nc, ctx, tag):
    sems = []

    @ctx.callback
    def _():
        if sems:
            nc.clear_and_free_semaphores(sems)
            nc.all_engine_barrier()

    def sem(n, lasting=False):
        s = nc.alloc_semaphore(f"{tag}_{n}")
        if not lasting:
            sems.append(s)
        return s

    return (lambda n, s, d: ctx.enter_context(nc.sbuf_tensor(f"{tag}_{n}", s, d)),
            lambda n, s, d: ctx.enter_context(nc.psum_tensor(f"{tag}_{n}", s, d)), sem)


def make_identity(nc, ident, tag):
    with ExitStack() as ctx:
        _, _, sem = alloc(nc, ctx, tag)
        zeroed, made = sem("zeroed"), sem("made")
        block = ctx.enter_context(nc.Block())

        @block.gpsimd
        def _(pool):
            nc.gpsimd.memset(ident[:], 0.0).then_inc(zeroed, 1)
            pool.wait_ge(zeroed, 1)
            nc.gpsimd.affine_select(out=ident[:], in_=ident[:], compare_op=ALU.not_equal, fill=1.0, base=0,
                                    pattern=[[-1, 128]], channel_multiplier=1).then_inc(made, 1)
            pool.wait_ge(made, 1)


def embed(nc, ids, tables, weights, biases, resid, ident, tag):
    with ExitStack() as ctx:
        sb, pm, sem = alloc(nc, ctx, tag)
        ids_i = sb("ids_i", [128, TILES], I32)
        ids_f = sb("ids_f", [128, TILES], F32)
        low = sb("low", [128, TILES], F32)
        index_f = sb("index_f", [128, TILES], F32)
        index = sb("index", [128, TILES, 3], I32)
        mask = sb("mask", [128, 3, TILES], F32)
        proj = sb("proj", [128, 3, DIM], F32)
        at_hand = [sb(f"at_hand{s}", [128, 3], I32) for s in range(2)]
        rows = [sb(f"rows{s}", [128, sum(EMB_DIMS)], F32) for s in range(2)]
        cat = [sb(f"cat{s}", [128, 384], F32) for s in range(2)]
        cat_t = [sb(f"cat_t{s}", [128, 3, 128], F32) for s in range(2)]
        ps_t = [pm(f"ps_t{s}", [128, 3, 128], F32) for s in range(2)]
        ps_e = [pm(f"ps_e{s}", [128, DIM], F32) for s in range(2)]
        ids_in, w_in = sem("ids_in"), sem("w_in")
        prep = sem("prep")
        gathered = [sem(f"gathered{s}", lasting=True) for s in range(2)]
        masked, masks, turned, copied, projected, stored = (
            sem(n) for n in ("masked", "masks", "turned", "copied", "projected", "stored"))
        PREP = 16
        block = ctx.enter_context(nc.Block())

        @block.sync
        def _(sp):
            sp.dma_start(ids_i[:], ids).then_inc(ids_in, 16)
            for k in range(HALVES):
                sp.dma_start(proj[:, k, :], weights[0][k * 128:(k + 1) * 128, :]).then_inc(w_in, 16)
            d1, d2 = EMB_DIMS[1], EMB_DIMS[2]
            sp.dma_start(proj[0:d1, 2, :], weights[1]).then_inc(w_in, 16)
            sp.dma_start(proj[d1:d1 + d2, 2, :], weights[2]).then_inc(w_in, 16)
            for k in range(3):
                sp.dma_start(proj[d1 + d2 + k:d1 + d2 + k + 1, 2, :], biases[k]).then_inc(w_in, 16)

        @block.vector
        def _(dve):
            dve.wait_ge(ids_in, 16)
            chain = Chain(dve, prep)
            chain.step(nc.vector.tensor_copy(ids_f[:], ids_i[:]))
            for k in range(3):
                lo, hi = CUTOFFS[k], CUTOFFS[k + 1]
                chain.step(nc.vector.tensor_scalar(low[:], ids_f[:], float(lo), None, ALU.is_ge))
                chain.step(nc.vector.scalar_tensor_tensor(mask[:, k, :], ids_f[:], float(hi), low[:], ALU.is_lt, ALU.mult))
                chain.step(nc.vector.tensor_scalar(index_f[:], ids_f[:], float(-lo), 0.0, ALU.add, ALU.max))
                chain.step(nc.vector.tensor_scalar(index[:, :, k], index_f[:], float(hi - lo - 1), None, ALU.min))
            for s in range(2):
                chain.step(nc.vector.memset(cat[s][:], 0.0))
            nc.vector.nop().then_inc(prep, PREP - chain.n)

            with dve.Fori(0, TILES // 2) as i:
                for s in range(2):
                    t = i * 2 + s
                    dve.wait_ge(gathered[s], i * 48 + 48)
                    dve.wait_ge(turned, t)
                    at = 0
                    for k, d in enumerate(EMB_DIMS):
                        nc.vector.tensor_scalar(cat[s][:, at:at + d], rows[s][:, at:at + d], mask[:, k, bass.ds(t, 1)],
                                                None, ALU.mult).then_inc(masked, 1)
                        at += d
                    nc.vector.tensor_copy(cat[s][:, at:at + 3], mask[:, :, bass.ds(t, 1)].rearrange("p k a -> p (k a)")
                                          ).then_inc(masked, 1)

        @block.gpsimd
        def _(pool):
            pool.wait_ge(prep, PREP)
            with pool.Fori(0, TILES // 2) as i:
                for s in range(2):
                    t = i * 2 + s
                    pool.wait_ge(masked, t * 4 + 4)
                    nc.gpsimd.tensor_copy(at_hand[s][:], index[:, bass.ds(t, 1), :].rearrange("p a k -> p (a k)")
                                          )
                    pool.drain()
                    at = 0
                    for k, d in enumerate(EMB_DIMS):
                        nc.gpsimd.indirect_dma_start(
                            rows[s][:, at:at + d], None, tables[k],
                            bass.IndirectOffsetOnAxis(ap=at_hand[s][:, k:k + 1], axis=0)).then_inc(gathered[s], 16)
                        at += d

        @block.tensor
        def _(pe):
            pe.wait_ge(w_in, 16 * (HALVES + 5))
            with pe.Fori(0, TILES // 2) as i:
                for s in range(2):
                    t = i * 2 + s
                    pe.wait_ge(masked, t * 4 + 4 + 8)
                    pe.wait_ge(copied, t)
                    for k in range(3):
                        m = nc.tensor.transpose(ps_t[s][:, k, :], cat[s][:, k * 128:(k + 1) * 128], ident[:])
                    m.then_inc(turned, 1)
                    pe.wait_ge(copied, t + 1)
                    pe.wait_ge(stored, t)
                    for k in range(3):
                        n = 128 if k < 2 else CAT - 256
                        m = nc.tensor.matmul(ps_e[s][:], cat_t[s][0:n, k, :], proj[0:n, k, :], start=k == 0, stop=k == 2)
                    m.then_inc(projected, 1)

        @block.scalar
        def _(act):
            nc.scalar.nop().then_inc(masked, 8)
            with act.Fori(0, TILES // 2) as i:
                for s in range(2):
                    t = i * 2 + s
                    act.wait_ge(turned, t + 1)
                    nc.scalar.copy(cat_t[s][:], ps_t[s][:]).then_inc(copied, 1)
                    act.wait_ge(projected, t + 1)
                    nc.scalar.mul(resid[:, bass.ds(t, 1), :].rearrange("p a d -> p (a d)"), ps_e[s][:], float(DIM) ** 0.5
                                  ).then_inc(stored, 1)


def norm_stats(nc, resid, mean, rstd, tag):
    with ExitStack() as ctx:
        sb, _, sem = alloc(nc, ctx, tag)
        stats = sb("stats", [128, TILES, 6], F32)
        a, b, var, root, inv = (sb(n, [128, TILES], F32) for n in ("a", "b", "var", "root", "inv"))
        rows_done, chained, root_done = sem("rows_done"), sem("chained"), sem("root_done")
        block = ctx.enter_context(nc.Block())

        @block.vector
        def _(dve):
            for t in range(TILES):
                nc.vector.bn_stats(stats[:, t, :], resid[:, t, :]).then_inc(rows_done, 1)
            dve.wait_ge(rows_done, TILES)
            chain = Chain(dve, chained)
            m0, v0, m1, v1 = (stats[:, :, k] for k in (1, 2, 4, 5))
            chain.step(nc.vector.tensor_tensor(a[:], m0, m1, ALU.subtract))
            chain.step(nc.vector.tensor_tensor(a[:], a[:], a[:], ALU.mult))
            chain.step(nc.vector.tensor_tensor(b[:], v0, v1, ALU.add))
            chain.step(nc.vector.tensor_scalar(b[:], b[:], 1.0 / DIM, EPS, ALU.mult, ALU.add))
            chain.step(nc.vector.scalar_tensor_tensor(var[:], a[:], 0.25, b[:], ALU.mult, ALU.add))
            chain.step(nc.vector.tensor_tensor(b[:], m0, m1, ALU.add))
            chain.step(nc.vector.tensor_scalar(mean[:], b[:], 0.5, None, ALU.mult))
            dve.wait_ge(root_done, 1)
            chain.step(nc.vector.reciprocal(inv[:], root[:]))
            chain.step(nc.vector.tensor_tensor(a[:], inv[:], inv[:], ALU.mult))
            chain.step(nc.vector.tensor_tensor(a[:], a[:], var[:], ALU.mult))
            chain.step(nc.vector.tensor_scalar(a[:], a[:], -0.5, 1.5, ALU.mult, ALU.add))
            chain.step(nc.vector.tensor_tensor(rstd[:], inv[:], a[:], ALU.mult))

        @block.scalar
        def _(act):
            act.wait_ge(chained, 5)
            nc.scalar.activation(root[:], var[:], ACT.Sqrt).then_inc(root_done, 1)


def project_qkv(nc, resid, mean, rstd, ident, parts_q, parts_k, values, w, tag):
    latent = "latent" in w
    with ExitStack() as ctx:
        sb, pm, sem = alloc(nc, ctx, tag)
        KD = LATENT if latent else 128
        KN = 1 if latent else HALVES
        wq = sb("wq", [128, HALVES, DIM], F32)
        wk = sb("wk", [KD, KN, DIM], F32)
        wv = sb("wv", [KD, KN, DIM], F32)
        if latent:
            wl = sb("wl", [128, HALVES, LATENT], F32)
            bias_qk = sb("bias_qk", [128, 2, HALVES], F32)
            bias_l = sb("bias_l", [LATENT, 1], F32)
            bias_v = sb("bias_v", [1, DIM], F32)
            ones = sb("ones", [1, 128], F32)
            lat = sb("lat", [LATENT, 512], F32)
        rows = sb("rows", [128, CHUNK, DIM], F32)
        rows_t = sb("rows_t", [128, HALVES, 512], F32)
        whole = [sb(f"whole{n}", [128, HALVES, 512], F32) for n in "qk"]
        rest = [sb(f"rest{n}", [128, HALVES, 512], F32) for n in "qk"]
        parts = [sb(f"parts{n}", [128, 3, HALVES, 512], BF16) for n in "qk"]
        ps_t = pm("ps_t", [128, HALVES, 512], F32)
        ps_qk = [pm(f"ps_{n}", [128, HALVES, 512], F32) for n in "qk"]
        ps_v = pm("ps_v", [128, CHUNK, DIM], F32)
        w_in, ones_set = sem("w_in"), sem("ones_set")
        normed, turned, copied, lat_done, lat_copied, v_done, v_stored = (
            sem(n) for n in ("normed", "turned", "copied", "lat_done", "lat_copied", "v_done", "v_stored"))
        done = [sem(f"{n}_done") for n in "qk"]
        out = [sem(f"{n}_out") for n in "qk"]
        split = [sem(f"{n}_split") for n in "qk"]
        stored = [sem(f"{n}_stored") for n in "qk"]
        CH = TILES // CHUNK // BATCH
        loads = []
        for k in range(HALVES):
            loads.append((wq[:, k, :], w["q"][k * 128:(k + 1) * 128, :]))
        for k in range(KN):
            loads.append((wk[:, k, :], w["k"][k * KD:(k + 1) * KD, :]))
            loads.append((wv[:, k, :], w["v"][k * KD:(k + 1) * KD, :]))
        if latent:
            for k in range(HALVES):
                loads.append((wl[:, k, :], w["latent"][k * 128:(k + 1) * 128, :]))
                loads.append((bias_qk[:, 0, k:k + 1], w["bq"][k].unsqueeze(1)))
                loads.append((bias_qk[:, 1, k:k + 1], w["bk"][k].unsqueeze(1)))
            loads.append((bias_l[:], w["bl"].unsqueeze(1)))
            loads.append((bias_v[:], w["bv"].unsqueeze(0)))
        block = ctx.enter_context(nc.Block())

        def every_chunk(eng, step):
            with eng.Fori(0, BATCH) as b:
                for c in range(CH):
                    step(b, c, b * CH + c)

        @block.sync
        def _(sp):
            for dst, src in loads:
                sp.dma_start(dst, src).then_inc(w_in, 16)

            def step(b, c, n):
                for x, dram in enumerate((parts_q, parts_k)):
                    sp.wait_ge(split[x], n * 4 + 4)
                    for part in range(3):
                        view = dram[part].rearrange("(b f h) d n -> b (h d) f n", b=BATCH, f=HALVES)
                        sp.dma_start(view[bass.ds(b, 1), :, :, c * 512:(c + 1) * 512].rearrange("b p f n -> (b p) f n"),
                                     parts[x][:, part, :, :]).then_inc(stored[x], 16)

            every_chunk(sp, step)
            for x in range(2):
                sp.wait_ge(stored[x], 48 * BATCH * CH)

        @block.vector
        def _(dve):
            if latent:
                nc.vector.memset(ones[:], 1.0).then_inc(ones_set, 1)

            def step(b, c, n):
                dve.wait_ge(turned, n)
                for j in range(CHUNK):
                    t = b * (CH * CHUNK) + (c * CHUNK + j)
                    nc.vector.tensor_scalar(rows[:, j, :], resid[:, bass.ds(t, 1), :].rearrange("p a d -> p (a d)"),
                                            mean[:, bass.ds(t, 1)], rstd[:, bass.ds(t, 1)], ALU.subtract, ALU.mult
                                            ).then_inc(normed, 1)
                for x in range(2):
                    dve.wait_ge(out[x], n + 1)
                    dve.wait_ge(stored[x], n * 48)
                    for k, op in enumerate((
                            lambda: nc.vector.tensor_copy(parts[x][:, 0, :, :], whole[x][:]),
                            lambda: nc.vector.tensor_tensor(rest[x][:], whole[x][:], parts[x][:, 0, :, :], ALU.subtract),
                            lambda: nc.vector.tensor_copy(parts[x][:, 1, :, :], rest[x][:]),
                            lambda: nc.vector.tensor_tensor(parts[x][:, 2, :, :], rest[x][:], parts[x][:, 1, :, :],
                                                            ALU.subtract))):
                        if k:
                            dve.wait_ge(split[x], n * 4 + k)
                        op().then_inc(split[x], 1)

            every_chunk(dve, step)

        @block.tensor
        def _(pe):
            pe.wait_ge(w_in, 16 * len(loads))
            if latent:
                pe.wait_ge(ones_set, 1)

            def step(b, c, n):
                pe.wait_ge(normed, n * CHUNK + CHUNK)
                pe.wait_ge(copied, n)
                for j in range(CHUNK):
                    for f in range(HALVES):
                        m = nc.tensor.transpose(ps_t[:, f, j * 128:(j + 1) * 128], rows[:, j, f * 128:(f + 1) * 128], ident[:])
                m.then_inc(turned, 1)
                pe.wait_ge(copied, n + 1)
                for x in range(2):
                    if x == 1 and latent:
                        pe.wait_ge(v_stored, n)
                        for k in range(HALVES):
                            m = nc.tensor.matmul(ps_v[0:LATENT, 0:2, :].rearrange("p a d -> p (a d)"), wl[:, k, :],
                                                 rows_t[:, k, :], start=k == 0, stop=k == HALVES - 1)
                        m.then_inc(lat_done, 1)
                        pe.wait_ge(lat_copied, n + 1)
                    pe.wait_ge(out[x], n)
                    for f in range(HALVES):
                        wx, src, kn = (wq, rows_t, HALVES) if x == 0 else (wk, rows_t, KN)
                        for k in range(kn):
                            rhs = lat[:] if x == 1 and latent else src[:, k, :]
                            m = nc.tensor.matmul(ps_qk[x][:, f, :], wx[:, k, f * 128:(f + 1) * 128], rhs,
                                                 start=k == 0, stop=k == kn - 1)
                    m.then_inc(done[x], 1)
                pe.wait_ge(v_stored, n)
                for j in range(CHUNK):
                    for k in range(KN):
                        src = lat[:, j * 128:(j + 1) * 128] if latent else rows_t[:, k, j * 128:(j + 1) * 128]
                        m = nc.tensor.matmul(ps_v[:, j, :], src, wv[:, k, :], start=k == 0,
                                             stop=k == KN - 1 and not latent)
                    if latent:
                        m = nc.tensor.matmul(ps_v[:, j, :], ones[:], bias_v[:], start=False, stop=True)
                m.then_inc(v_done, 1)

            every_chunk(pe, step)

        @block.scalar
        def _(act):
            act.wait_ge(w_in, 16 * len(loads))

            def step(b, c, n):
                act.wait_ge(turned, n + 1)
                nc.scalar.copy(rows_t[:], ps_t[:]).then_inc(copied, 1)
                for x in range(2):
                    if x == 1 and latent:
                        act.wait_ge(lat_done, n + 1)
                        nc.scalar.activation(lat[:], ps_v[0:LATENT, 0:2, :].rearrange("p a d -> p (a d)"), ACT.Identity,
                                             bias=bias_l[:]).then_inc(lat_copied, 1)
                    act.wait_ge(done[x], n + 1)
                    act.wait_ge(split[x], n * 4)
                    if latent:
                        for f in range(HALVES):
                            m = nc.scalar.activation(whole[x][:, f, :], ps_qk[x][:, f, :], ACT.Identity,
                                                     bias=bias_qk[:, x, f:f + 1])
                        m.then_inc(out[x], 1)
                    else:
                        nc.scalar.copy(whole[x][:], ps_qk[x][:]).then_inc(out[x], 1)
                act.wait_ge(v_done, n + 1)
                for j in range(CHUNK):
                    m = nc.scalar.copy(values[:, bass.ds(b * HEADS, HEADS), c * CHUNK + j, :],
                                       ps_v[:, j, :].rearrange("p (h d) -> p h d", d=HEAD_DIM))
                m.then_inc(v_stored, 1)

            every_chunk(act, step)


def project_out(nc, resid, attended, ident, w_out, b_out, tag):
    with ExitStack() as ctx:
        sb, pm, sem = alloc(nc, ctx, tag)
        wo = sb("wo", [128, HALVES, DIM], F32)
        bo = sb("bo", [1, DIM], F32)
        ones = sb("ones", [1, 128], F32)
        rows = [sb(f"rows{s}", [128, CHUNK, DIM], F32) for s in range(2)]
        rows_t = [sb(f"rows_t{s}", [128, HALVES, 512], F32) for s in range(2)]
        ps_t = [pm(f"ps_t{s}", [128, HALVES, 512], F32) for s in range(2)]
        ps_y = [pm(f"ps_y{s}", [128, CHUNK, DIM], F32) for s in range(2)]
        w_in, ones_set, staged, turned, copied, done, added = (
            sem(n) for n in ("w_in", "ones_set", "staged", "turned", "copied", "done", "added"))
        CH = TILES // CHUNK // BATCH
        block = ctx.enter_context(nc.Block())

        def every_chunk(eng, step):
            with eng.Fori(0, BATCH) as b:
                for c in range(CH):
                    step(b, c, b * CH + c, c % 2)

        @block.sync
        def _(sp):
            for k in range(HALVES):
                sp.dma_start(wo[:, k, :], w_out[k * 128:(k + 1) * 128, :]).then_inc(w_in, 16)
            sp.dma_start(bo[:], b_out.unsqueeze(0)).then_inc(w_in, 16)

        @block.gpsimd
        def _(pool):
            def step(b, c, n, s):
                pool.wait_ge(turned, n)
                for j in range(CHUNK):
                    m = nc.gpsimd.tensor_copy(rows[s][:, j, :].rearrange("p (h d) -> p h d", d=HEAD_DIM),
                                              attended[:, bass.ds(b * HEADS, HEADS), c * CHUNK + j, :])
                    m.then_inc(staged, 1)

            every_chunk(pool, step)

        @block.tensor
        def _(pe):
            pe.wait_ge(w_in, 16 * (HALVES + 1))
            pe.wait_ge(ones_set, 1)

            def step(b, c, n, s):
                pe.wait_ge(staged, n * CHUNK + CHUNK)
                for j in range(CHUNK):
                    for f in range(HALVES):
                        m = nc.tensor.transpose(ps_t[s][:, f, j * 128:(j + 1) * 128], rows[s][:, j, f * 128:(f + 1) * 128],
                                                ident[:])
                m.then_inc(turned, 1)
                pe.wait_ge(copied, n + 1)
                pe.wait_ge(added, n)
                for j in range(CHUNK):
                    for k in range(HALVES):
                        nc.tensor.matmul(ps_y[s][:, j, :], rows_t[s][:, k, j * 128:(j + 1) * 128], wo[:, k, :],
                                         start=k == 0, stop=False)
                    m = nc.tensor.matmul(ps_y[s][:, j, :], ones[:], bo[:], start=False, stop=True)
                m.then_inc(done, 1)

            every_chunk(pe, step)

        @block.scalar
        def _(act):
            def step(b, c, n, s):
                act.wait_ge(turned, n + 1)
                nc.scalar.copy(rows_t[s][:], ps_t[s][:]).then_inc(copied, 1)

            every_chunk(act, step)

        @block.vector
        def _(dve):
            nc.vector.memset(ones[:], 1.0).then_inc(ones_set, 1)

            def step(b, c, n, s):
                dve.wait_ge(done, n + 1)
                into = resid[:, bass.ds(b * (CH * CHUNK) + c * CHUNK, CHUNK), :]
                nc.vector.tensor_tensor(into, into, ps_y[s][:], ALU.add).then_inc(added, 1)

            every_chunk(dve, step)


def alibi_rows():
    slopes = np.array([1.0 / (256 ** (1.0 / HEADS)) ** (h + 1) for h in range(HEADS)], np.float32)
    rest = (slopes[:, None].astype(np.float64) * np.arange(SEQ)[None, :] / 4)
    bits = np.zeros((2, PAIRS, 6, SEQ), np.uint16)
    one, sign = np.uint16(0x3F80), np.uint16(0x8000)
    bits[0, :, 0:3], bits[1, :, 3:6] = one, one
    for part in range(3):
        top = (rest.astype(np.float32).view(np.uint32) >> 16).astype(np.uint16)
        rest = rest - (top.astype(np.uint32) << 16).view(np.float32)
        for b in range(BATCH):
            bits[0, b * HEADS:(b + 1) * HEADS, 3 + part] = top | sign
            bits[1, b * HEADS:(b + 1) * HEADS, part] = top
    return bits


def attention_layer(nc, resid, ident, w, w_out, b_out, alibi, scale, tag):
    shape = (3, PAIRS, HEAD_DIM, SEQ)
    parts_q = nc.dram_tensor(f"{tag}_parts_q", shape, BF16).ap()
    parts_k = nc.dram_tensor(f"{tag}_parts_k", shape, BF16).ap()
    with ExitStack() as ctx:
        sb, _, _ = alloc(nc, ctx, tag)
        values = sb("values", [128, PAIRS, SEQ // 128, HEAD_DIM], F32)
        attended = sb("attended", [128, PAIRS, SEQ // 128, HEAD_DIM], F32)
        mean, rstd = sb("mean", [128, TILES], F32), sb("rstd", [128, TILES], F32)
        norm_stats(nc, resid, mean, rstd, tag + "n")
        project_qkv(nc, resid, mean, rstd, ident, parts_q, parts_k, values, w, tag + "p")
        rows = None if alibi is None else (alibi[0].bitcast(BF16), alibi[1].bitcast(BF16))
        attention_core(nc, parts_q, parts_k, values, attended, rows, scale, PAIRS, tag + "c")
        project_out(nc, resid, attended, ident, w_out, b_out, tag + "o")


def gate(nc, resid, mean, rstd, ident, gate_w, gate_b, rows_out, logits, tag):
    with ExitStack() as ctx:
        sb, pm, sem = alloc(nc, ctx, tag)
        gw = sb("gw", [128, HALVES, EXPERTS], F32)
        gb = sb("gb", [1, EXPERTS], F32)
        ones = sb("ones", [1, 128], F32)
        rows = [sb(f"rows{s}", [128, CHUNK, DIM], F32) for s in range(2)]
        rows_t = [sb(f"rows_t{s}", [128, HALVES, 512], F32) for s in range(2)]
        ps_t = [pm(f"ps_t{s}", [128, HALVES, 512], F32) for s in range(2)]
        ps_g = [pm(f"ps_g{s}", [128, CHUNK, EXPERTS], F32) for s in range(2)]
        w_in, ones_set, normed, turned, copied, done, kept = (
            sem(n) for n in ("w_in", "ones_set", "normed", "turned", "copied", "done", "kept"))
        rows_stored = [sem(f"rows_stored{s}") for s in range(2)]
        CH = TILES // CHUNK
        block = ctx.enter_context(nc.Block())

        def every_chunk(eng, step):
            with eng.Fori(0, CH // 2) as i:
                for s in range(2):
                    step(i, i * 2 + s, s)

        @block.sync
        def _(sp):
            for k in range(HALVES):
                sp.dma_start(gw[:, k, :], gate_w[k * 128:(k + 1) * 128, :]).then_inc(w_in, 16)
            sp.dma_start(gb[:], gate_b.unsqueeze(0)).then_inc(w_in, 16)
            view = rows_out.rearrange("(t p) d -> p t d", p=128)

            def step(i, n, s):
                sp.wait_ge(normed, n * CHUNK + CHUNK)
                sp.dma_start(view[:, bass.ds(n * CHUNK, CHUNK), :], rows[s][:]).then_inc(rows_stored[s], 16)

            every_chunk(sp, step)
            for s in range(2):
                sp.wait_ge(rows_stored[s], 16 * (CH // 2))

        @block.vector
        def _(dve):
            nc.vector.memset(ones[:], 1.0).then_inc(ones_set, 1)

            def step(i, n, s):
                dve.wait_ge(turned, n)
                dve.wait_ge(rows_stored[s], i * 16)
                for j in range(CHUNK):
                    t = n * CHUNK + j
                    nc.vector.tensor_scalar(rows[s][:, j, :], resid[:, bass.ds(t, 1), :].rearrange("p a d -> p (a d)"),
                                            mean[:, bass.ds(t, 1)], rstd[:, bass.ds(t, 1)], ALU.subtract, ALU.mult
                                            ).then_inc(normed, 1)

            every_chunk(dve, step)

        @block.tensor
        def _(pe):
            pe.wait_ge(w_in, 16 * (HALVES + 1))
            pe.wait_ge(ones_set, 1)

            def step(i, n, s):
                pe.wait_ge(normed, n * CHUNK + CHUNK)
                for j in range(CHUNK):
                    for f in range(HALVES):
                        m = nc.tensor.transpose(ps_t[s][:, f, j * 128:(j + 1) * 128], rows[s][:, j, f * 128:(f + 1) * 128],
                                                ident[:])
                m.then_inc(turned, 1)
                pe.wait_ge(copied, n + 1)
                pe.wait_ge(kept, n)
                for j in range(CHUNK):
                    for k in range(HALVES):
                        nc.tensor.matmul(ps_g[s][:, j, :], rows_t[s][:, k, j * 128:(j + 1) * 128], gw[:, k, :],
                                         start=k == 0, stop=False)
                    m = nc.tensor.matmul(ps_g[s][:, j, :], ones[:], gb[:], start=False, stop=True)
                m.then_inc(done, 1)

            every_chunk(pe, step)

        @block.scalar
        def _(act):
            def step(i, n, s):
                act.wait_ge(turned, n + 1)
                nc.scalar.copy(rows_t[s][:], ps_t[s][:]).then_inc(copied, 1)
                act.wait_ge(done, n + 1)
                nc.scalar.copy(logits[:, bass.ds(n * CHUNK, CHUNK), :], ps_g[s][:]).then_inc(kept, 1)

            every_chunk(act, step)


def route(nc, logits, weight, slots, slot_token, block_rows, tag):
    with ExitStack() as ctx:
        sb, pm, sem = alloc(nc, ctx, tag)
        E3 = [128, TILES, EXPERTS]
        NS = BLOCKS * SUBS
        prob, z, tie, eq, pick1, pick2, chosen = (sb(n, E3, F32) for n in (
            "prob", "z", "tie", "eq", "pick1", "pick2", "chosen"))
        totals, upto, pos, hit = (sb(n, E3, F32) for n in ("totals", "upto", "pos", "hit"))
        top, total, inv, cand = (sb(n, [128, TILES], F32) for n in ("top", "total", "inv", "cand"))
        best = [sb(f"best{k}", [128, TILES], F32) for k in range(2)]
        slot_f = [sb(f"slot_f{k}", [128, TILES], F32) for k in range(2)]
        part_i = sb("part_i", [128, TILES, 2], I32)
        low = sb("low", [128, TILES, 2], F32)
        high = sb("high", [128, TILES, 2], F32)
        ones = sb("ones", [128, 128], F32)
        before = sb("before", [128, 128], F32)
        fill = sb("fill", [128, EXPERTS, TOKENS // BLOCK], F32)
        full = sb("full", [128, EXPERTS, TOKENS // BLOCK], F32)
        blocks, ends, base = (sb(n, [128, EXPERTS], F32) for n in ("blocks", "ends", "base"))
        block_no = sb("block_no", [128, BLOCKS, EXPERTS], F32)
        past = sb("past", [128, BLOCKS, EXPERTS], F32)
        expert = sb("expert", [128, BLOCKS], F32)
        lane = sb("lane", [128, 1], F32)
        column = sb("column", [128, 128], F32)
        token = sb("token", [128, TILES], F32)
        low_hot = [sb(f"low_hot{s}", [128, 128], F32) for s in range(2)]
        high_hot = [sb(f"high_hot{s}", [128, NS], F32) for s in range(2)]
        ps_rank = pm("ps_rank", E3, F32)
        ps_total = pm("ps_total", E3, F32)
        ps_slot = pm("ps_slot", [128, NS], F32)
        consts, chained, exp_done, counted, hot, used, made = (
            sem(n) for n in ("consts", "chained", "exp_done", "counted", "hot", "used", "made"))
        block = ctx.enter_context(nc.Block())
        marks = {}

        @block.gpsimd
        def _(pool):
            io = dict(allow_small_or_imprecise_dtypes=True)
            nc.gpsimd.iota(tie[:], pattern=[[0, TILES], [-1, EXPERTS]], base=EXPERTS, channel_multiplier=0, **io).then_inc(consts, 1)
            nc.gpsimd.iota(fill[:], pattern=[[0, EXPERTS], [BLOCK, TOKENS // BLOCK]], base=0, channel_multiplier=0, **io).then_inc(consts, 1)
            nc.gpsimd.iota(block_no[:], pattern=[[1, BLOCKS], [0, EXPERTS]], base=0, channel_multiplier=0, **io).then_inc(consts, 1)
            nc.gpsimd.iota(lane[:], pattern=[[0, 1]], base=0, channel_multiplier=1, **io).then_inc(consts, 1)
            nc.gpsimd.iota(column[:], pattern=[[1, 128]], base=0, channel_multiplier=0, **io).then_inc(consts, 1)
            nc.gpsimd.iota(token[:], pattern=[[128, TILES]], base=0, channel_multiplier=1, **io).then_inc(consts, 1)

        @block.vector
        def _(dve):
            dve.wait_ge(consts, 6)
            chain = Chain(dve, chained)
            do = chain.step
            v = nc.vector
            wide = lambda x: x[:].unsqueeze(2).to_broadcast(E3)
            do(v.memset(ones[:], 1.0))
            do(v.tensor_scalar(before[:], column[:], lane[:], None, ALU.is_gt))
            do(v.tensor_reduce(top[:], logits[:], AX.X, ALU.max))
            do(v.tensor_tensor(z[:], logits[:], wide(top), ALU.subtract))
            marks["z"] = chain.n
            dve.wait_ge(exp_done, 1)
            do(v.tensor_reduce(total[:], prob[:], AX.X, ALU.add))
            do(v.reciprocal(inv[:], total[:]))
            do(v.tensor_tensor(prob[:], prob[:], wide(inv), ALU.mult))
            for k, pick in enumerate((pick1, pick2)):
                do(v.tensor_reduce(best[k][:], prob[:], AX.X, ALU.max))
                do(v.tensor_tensor(eq[:], prob[:], wide(best[k]), ALU.is_equal))
                do(v.tensor_tensor(eq[:], eq[:], tie[:], ALU.mult))
                do(v.tensor_reduce(cand[:], eq[:], AX.X, ALU.max))
                do(v.tensor_tensor(pick[:], eq[:], wide(cand), ALU.is_equal))
                if k == 0:
                    do(v.scalar_tensor_tensor(prob[:], pick[:], -4.0, prob[:], ALU.mult, ALU.add))
            do(v.tensor_tensor(chosen[:], pick1[:], pick2[:], ALU.add))
            marks["chosen"] = chain.n
            do(v.tensor_tensor(total[:], best[0][:], best[1][:], ALU.add))
            do(v.tensor_scalar(total[:], total[:], 1e-20, None, ALU.add))
            do(v.reciprocal(inv[:], total[:]))
            for k in range(2):
                do(v.tensor_tensor(weight[:, :, k], best[k][:], inv[:], ALU.mult))
            dve.wait_ge(counted, 1)
            do(v.tensor_copy(totals[:], ps_total[:]))
            for e in range(EXPERTS):
                do(v.tensor_tensor_scan(upto[:, :, e], ones[:, 0:TILES], totals[:, :, e], 0.0, ALU.mult, ALU.add))
            count = upto[:, TILES - 1, :].unsqueeze(2).to_broadcast([128, EXPERTS, TOKENS // BLOCK])
            do(v.tensor_tensor(full[:], count, fill[:], ALU.is_gt))
            do(v.tensor_reduce(blocks[:], full[:], AX.X, ALU.add))
            do(v.tensor_tensor_scan(ends[:], ones[:, 0:EXPERTS], blocks[:], 0.0, ALU.mult, ALU.add))
            do(v.tensor_tensor(base[:], ends[:], blocks[:], ALU.subtract))
            do(v.tensor_scalar(base[:], base[:], float(BLOCK), None, ALU.mult))
            do(v.tensor_tensor(pos[:], upto[:], totals[:], ALU.subtract))
            do(v.tensor_tensor(pos[:], pos[:], ps_rank[:], ALU.add))
            do(v.tensor_tensor(pos[:], pos[:], base[:].unsqueeze(1).to_broadcast(E3), ALU.add))
            for k, pick in enumerate((pick1, pick2)):
                do(v.tensor_tensor(hit[:], pick[:], pos[:], ALU.mult))
                do(v.tensor_reduce(slot_f[k][:], hit[:], AX.X, ALU.add))
                do(v.tensor_copy(slots[:, :, k], slot_f[k][:]))
            do(v.tensor_tensor(past[:], block_no[:], ends[:].unsqueeze(1).to_broadcast([128, BLOCKS, EXPERTS]), ALU.is_ge))
            do(v.tensor_reduce(expert[:], past[:], AX.X, ALU.add))
            do(v.tensor_scalar(expert[:], expert[:], float(EXPERTS - 1), 128.0, ALU.min, ALU.mult))
            do(v.tensor_scalar(block_rows[:], expert[:], lane[:], None, ALU.add))
            do(v.tensor_scalar(part_i[:], slots[:], 7, None, ALU.logical_shift_right))
            do(v.tensor_copy(high[:], part_i[:]))
            do(v.tensor_scalar(part_i[:], slots[:], 127, None, ALU.bitwise_and))
            do(v.tensor_copy(low[:], part_i[:]))
            with dve.Fori(0, TILES) as t:
                for k in range(2):
                    dve.wait_ge(used, t * 2 + k)
                    v.tensor_scalar(low_hot[k][:], column[:], low[:, bass.ds(t, 1), k], token[:, bass.ds(t, 1)],
                                    ALU.is_equal, ALU.mult).then_inc(hot, 1)
                    v.tensor_scalar(high_hot[k][:], column[:, 0:NS], high[:, bass.ds(t, 1), k], None,
                                    ALU.is_equal).then_inc(hot, 1)
            dve.wait_ge(used, 2 * TILES)
            do(v.tensor_copy(slot_token[:], ps_slot[:]))

        @block.scalar
        def _(act):
            act.wait_ge(chained, marks["z"])
            nc.scalar.activation(prob[:], z[:], ACT.Exp).then_inc(exp_done, 1)

        @block.tensor
        def _(pe):
            pe.wait_ge(chained, marks["chosen"])
            nc.tensor.matmul(ps_rank[:], before[:], chosen[:], start=True, stop=True)
            nc.tensor.matmul(ps_total[:], ones[:], chosen[:], start=True, stop=True).then_inc(counted, 1)

            def add(t, k, first, last):
                pe.wait_ge(hot, t * 4 + 2 * k + 2)
                nc.tensor.matmul(ps_slot[:], low_hot[k][:], high_hot[k][:], start=first, stop=last).then_inc(used, 1)

            add(0, 0, True, False)
            add(0, 1, False, False)
            with pe.Fori(1, TILES - 1) as t:
                for k in range(2):
                    add(t, k, False, False)
            add(TILES - 1, 0, False, False)
            add(TILES - 1, 1, False, True)


def experts(nc, rows_in, table, slot_token, block_rows, slot_out, ident, tag):
    with ExitStack() as ctx:
        sb, pm, sem = alloc(nc, ctx, tag)
        which = [sb(f"which{s}", [128, SUBS + 1], I32) for s in range(2)]
        wts = [sb(f"wts{s}", [128, EROW], F32) for s in range(2)]
        rows = [sb(f"rows{s}", [128, SUBS, DIM], F32) for s in range(2)]
        rows_t = [sb(f"rows_t{s}", [128, HALVES, BLOCK], F32) for s in range(2)]
        gated = [sb(f"gated{s}", [128, BLOCK], F32) for s in range(2)]
        prod = [sb(f"prod{s}", [128, BLOCK], F32) for s in range(2)]
        hid = [sb(f"hid{s}", [128, FT, BLOCK], F32) for s in range(2)]
        outs = [sb(f"outs{s}", [128, SUBS, DIM], F32) for s in range(2)]
        ps_t = pm("ps_t", [128, HALVES, BLOCK], F32)
        ps_h = [pm(f"ps_h{s}", [128, 2, BLOCK], F32) for s in range(3)]
        ps_y = [pm(f"ps_y{s}", [128, SUBS, DIM], F32) for s in range(2)]
        ones_set, staged, turned, copied, scored, gate_out, prod_out, hid_out, down_done, outs_out = (
            sem(n) for n in ("ones_set", "staged", "turned", "copied", "scored", "gate_out", "prod_out", "hid_out",
                             "down_done", "outs_out"))
        w_in = [sem(f"w_in{s}", lasting=True) for s in range(2)]
        x_in = [sem(f"x_in{s}", lasting=True) for s in range(2)]
        y_out = [sem(f"y_out{s}") for s in range(2)]
        block = ctx.enter_context(nc.Block())
        PARTS = [(m, 128 if m < FT - 1 else FREST) for m in range(FT)]

        def every_block(eng, step):
            with eng.Fori(0, BLOCKS // 2) as i:
                for s in range(2):
                    step(i, i * 2 + s, s)

        @block.gpsimd
        def _(pool):
            def step(i, n, s):
                pool.wait_ge(down_done, n)
                nc.gpsimd.tensor_copy(which[s][:, 0:1], block_rows[:, bass.ds(n, 1)])
                nc.gpsimd.tensor_copy(which[s][:, 1:1 + SUBS], slot_token[:, bass.ds(n * SUBS, SUBS)])
                pool.drain()
                for j in range(SUBS):
                    nc.gpsimd.indirect_dma_start(rows[s][:, j, :], None, rows_in, bass.IndirectOffsetOnAxis(
                        ap=which[s][:, 1 + j:2 + j], axis=0)).then_inc(x_in[s], 16)
                nc.gpsimd.indirect_dma_start(wts[s][:], None, table, bass.IndirectOffsetOnAxis(
                    ap=which[s][:, 0:1], axis=0)).then_inc(w_in[s], 16)

            every_block(pool, step)

        @block.tensor
        def _(pe):
            nc.tensor.nop().then_inc(down_done, 1)

            def down(i, n, s):
                pe.wait_ge(hid_out, n * FT + FT)
                pe.wait_ge(outs_out, n - 1 if isinstance(n, int) else n)
                for j in range(SUBS):
                    for m, size in PARTS:
                        k = size if m < FT - 1 else size + 1
                        mm = nc.tensor.matmul(ps_y[s][:, j, :], hid[s][0:k, m, j * 128:(j + 1) * 128],
                                              wts[s][0:k, DOWN + m * DIM:DOWN + (m + 1) * DIM], start=m == 0, stop=m == FT - 1)
                mm.then_inc(down_done, 1)

            def step(i, n, s):
                pe.wait_ge(x_in[s], i * 16 * SUBS + 16 * SUBS)
                pe.wait_ge(copied, n)
                for j in range(SUBS):
                    for f in range(HALVES):
                        mm = nc.tensor.transpose(ps_t[:, f, j * 128:(j + 1) * 128], rows[s][:, j, f * 128:(f + 1) * 128],
                                                 ident[:])
                mm.then_inc(turned, 1)
                pe.wait_ge(w_in[s], i * 16 + 16)
                pe.wait_ge(copied, n + 1)
                for m, size in PARTS:
                    pe.wait_ge(prod_out, n * FT + m)
                    for x, at in ((0, UP), (1, GATE)):
                        for k in range(HALVES):
                            c = at + k * FFN + m * 128
                            mm = nc.tensor.matmul(ps_h[m % 3][0:size, x, :], wts[s][:, c:c + size], rows_t[s][:, k, :],
                                                  start=k == 0, stop=k == HALVES - 1)
                    mm.then_inc(scored, 1)

            step(0, 0, 0)
            with pe.Fori(0, BLOCKS // 2 - 1) as i:
                step(i, i * 2 + 1, 1)
                down(i, i * 2, 0)
                step(i + 1, i * 2 + 2, 0)
                down(i, i * 2 + 1, 1)
            last = BLOCKS // 2 - 1
            step(last, BLOCKS - 1, 1)
            down(last, BLOCKS - 2, 0)
            down(last, BLOCKS - 1, 1)

        @block.scalar
        def _(act):
            nc.scalar.nop().then_inc(outs_out, 1)
            act.wait_ge(ones_set, 2)

            def step(i, n, s):
                act.wait_ge(turned, n + 1)
                nc.scalar.copy(rows_t[s][:], ps_t[:]).then_inc(copied, 1)
                act.wait_ge(w_in[s], i * 16 + 16)
                for m, size in PARTS:
                    act.wait_ge(scored, n * FT + m + 1)
                    act.wait_ge(prod_out, n * FT + m)
                    nc.scalar.activation(gated[m % 2][0:size, :], ps_h[m % 3][0:size, 1, :], ACT.Identity,
                                         bias=wts[s][0:size, GATEB + m:GATEB + m + 1]).then_inc(gate_out, 1)
                    if m:
                        silu(i, n, s, m - 1)
                silu(i, n, s, FT - 1)

            def silu(i, n, s, m):
                size = PARTS[m][1]
                act.wait_ge(prod_out, n * FT + m + 3)
                if m == 0:
                    act.wait_ge(down_done, n)
                nc.scalar.activation(hid[s][0:size, m, :], prod[m % 2][0:size, :], ACT.Silu).then_inc(hid_out, 1)

            every_block(act, step)

        @block.vector
        def _(dve):
            for s in range(2):
                nc.vector.memset(hid[s][0:64, FT - 1, :], 1.0).then_inc(ones_set, 1)
            nc.vector.nop().then_inc(prod_out, 2)

            def step(i, n, s):
                dve.wait_ge(w_in[s], i * 16 + 16)
                for m, size in PARTS:
                    dve.wait_ge(gate_out, n * FT + m + 1)
                    dve.wait_ge(hid_out, n * FT + m - 1 if m else n * FT)
                    nc.vector.scalar_tensor_tensor(prod[m % 2][0:size, :], ps_h[m % 3][0:size, 0, :],
                                                   wts[s][0:size, UPB + m:UPB + m + 1], gated[m % 2][0:size, :],
                                                   ALU.add, ALU.mult).then_inc(prod_out, 1)

            def finish(i, n, s):
                dve.wait_ge(down_done, n + 2)
                dve.wait_ge(y_out[s], i * 16)
                nc.vector.tensor_copy(outs[s][:], ps_y[s][:]).then_inc(outs_out, 1)

            step(0, 0, 0)
            with dve.Fori(0, BLOCKS // 2 - 1) as i:
                step(i, i * 2 + 1, 1)
                finish(i, i * 2, 0)
                step(i + 1, i * 2 + 2, 0)
                finish(i, i * 2 + 1, 1)
            last = BLOCKS // 2 - 1
            step(last, BLOCKS - 1, 1)
            finish(last, BLOCKS - 2, 0)
            finish(last, BLOCKS - 1, 1)

        @block.sync
        def _(sp):
            view = slot_out.rearrange("(n j p) d -> p n j d", p=128, j=SUBS)

            def step(i, n, s):
                sp.wait_ge(outs_out, n + 2)
                sp.dma_start(view[:, bass.ds(n, 1), :, :].rearrange("p a j d -> p (a j) d"), outs[s][:]
                             ).then_inc(y_out[s], 16)

            every_block(sp, step)
            for s in range(2):
                sp.wait_ge(y_out[s], 16 * (BLOCKS // 2))


def combine(nc, resid, slots, weight, slot_out, tag):
    with ExitStack() as ctx:
        sb, _, sem = alloc(nc, ctx, tag)
        N = 4
        which = [sb(f"which{s}", [128, 2], I32) for s in range(N)]
        got = [sb(f"got{s}", [128, 2, DIM], F32) for s in range(N)]
        gathered = [sem(f"gathered{s}", lasting=True) for s in range(N)]
        added = sem("added")
        block = ctx.enter_context(nc.Block())

        @block.gpsimd
        def _(pool):
            with pool.Fori(0, TILES // N) as i:
                for s in range(N):
                    pool.wait_ge(added, i * (2 * N) + 2 * s + 2)
                    nc.gpsimd.tensor_copy(which[s][:], slots[:, bass.ds(i * N + s, 1), :].rearrange("p a k -> p (a k)"))
                    pool.drain()
                    for k in range(2):
                        nc.gpsimd.indirect_dma_start(got[s][:, k, :], None, slot_out, bass.IndirectOffsetOnAxis(
                            ap=which[s][:, k:k + 1], axis=0)).then_inc(gathered[s], 16)

        @block.vector
        def _(dve):
            nc.vector.nop().then_inc(added, 2 * N)
            with dve.Fori(0, TILES // N) as i:
                for s in range(N):
                    t = i * N + s
                    dve.wait_ge(gathered[s], i * 32 + 32)
                    row = resid[:, bass.ds(t, 1), :].rearrange("p a d -> p (a d)")
                    for k in range(2):
                        if k:
                            dve.wait_ge(added, t * 2 + 1 + 2 * N)
                        nc.vector.scalar_tensor_tensor(row, got[s][:, k, :], weight[:, bass.ds(t, 1), k], row,
                                                       ALU.mult, ALU.add).then_inc(added, 1)


def moe_layer(nc, resid, ident, a, tag):
    rows = nc.dram_tensor(f"{tag}_rows", (TOKENS, DIM), F32).ap()
    slot_out = nc.dram_tensor(f"{tag}_slot_out", (BLOCKS * BLOCK, DIM), F32).ap()
    with ExitStack() as ctx:
        sb, _, _ = alloc(nc, ctx, tag)
        mean, rstd = sb("mean", [128, TILES], F32), sb("rstd", [128, TILES], F32)
        logits = sb("logits", [128, TILES, EXPERTS], F32)
        weight = sb("weight", [128, TILES, 2], F32)
        slots = sb("slots", [128, TILES, 2], I32)
        slot_token = sb("slot_token", [128, BLOCKS * SUBS], I32)
        block_rows = sb("block_rows", [128, BLOCKS], I32)
        norm_stats(nc, resid, mean, rstd, tag + "n")
        gate(nc, resid, mean, rstd, ident, a["gate_w"], a["gate_b"], rows, logits, tag + "g")
        route(nc, logits, weight, slots, slot_token, block_rows, tag + "r")
        experts(nc, rows, a["experts"], slot_token, block_rows, slot_out, ident, tag + "e")
        combine(nc, resid, slots, weight, slot_out, tag + "c")


def moe_arrays(z):
    C = np.ascontiguousarray
    g = lambda k: np.asarray(z["L0_ffn_" + k])
    out = np.zeros((EXPERTS, 128, EROW), np.float32)
    for at, name in ((UP, "up"), (GATE, "gp")):
        w = g(name + "_w").reshape(EXPERTS, FFN, HALVES, 128).transpose(0, 3, 2, 1)
        out[:, :, at:at + HALVES * FFN] = w.reshape(EXPERTS, 128, HALVES * FFN)
    down = g("down_w").transpose(0, 2, 1)
    for m in range(FT):
        size = 128 if m < FT - 1 else FREST
        out[:, 0:size, DOWN + m * DIM:DOWN + (m + 1) * DIM] = down[:, m * 128:m * 128 + size]
        for at, name in ((UPB, "up_b"), (GATEB, "gp_b")):
            out[:, 0:size, at + m] = g(name)[:, m * 128:m * 128 + size]
    out[:, FREST, DOWN + (FT - 1) * DIM:DOWN + FT * DIM] = g("down_b")
    return {"experts": out.reshape(EXPERTS * 128, EROW), "gate_w": C(g("gate_w").T), "gate_b": C(g("gate_b"))}


MAGIC = 1.5 * 2.0 ** 23
DOWNWARDS = 1.0 - 2.0 ** -23


class Fp4:

    STEPS = 14

    def __init__(self, nc, sb, name, n):
        blocks = n // QUANT
        self.nc, self.n = nc, n
        self.peak, self.scale, self.inv = (sb(f"{name}_{k}", [128, blocks], F32) for k in ("peak", "scale", "inv"))
        self.a, self.b, self.c = (sb(f"{name}_{k}", [128, n], F32) for k in "abc")

    def run(self, eng, sem, base, x, out, last=None):
        v, n = self.nc.vector, self.n
        wide = lambda s: s[:].unsqueeze(2).to_broadcast([128, n // QUANT, QUANT])
        grouped = lambda t: t.rearrange("p (g q) -> p g q", q=QUANT)
        a, b, c = self.a[:], self.b[:], self.c[:]
        I = lambda t: t.bitcast(I32)
        ops = (
            lambda: v.tensor_reduce(self.peak[:], grouped(x), AX.X, ALU.max, apply_absolute_value=True),
            lambda: v.tensor_scalar(self.scale[:], self.peak[:], 1.0 / 6.0, 1e-12, ALU.mult, ALU.max),
            lambda: v.reciprocal(self.inv[:], self.scale[:]),
            lambda: v.tensor_scalar(self.inv[:], self.inv[:], DOWNWARDS, None, ALU.mult),
            lambda: v.tensor_tensor(grouped(a), grouped(x), wide(self.inv), ALU.mult),
            lambda: v.tensor_scalar(I(a), I(a), 0x7FFFFFFF, None, ALU.bitwise_and),
            lambda: v.tensor_scalar(b, a, 2.0, 4.0, ALU.max, ALU.min),
            lambda: v.tensor_scalar(b, b, MAGIC, MAGIC + 6.0, ALU.add, ALU.subtract),
            lambda: v.tensor_scalar(c, a, 2.0, MAGIC / 2, ALU.min, ALU.add),
            lambda: v.scalar_tensor_tensor(b, c, -MAGIC / 2, b, ALU.add, ALU.add),
            lambda: v.tensor_scalar(c, a, 4.0, MAGIC * 2, ALU.max, ALU.add),
            lambda: v.scalar_tensor_tensor(b, c, -MAGIC * 2, b, ALU.add, ALU.add),
            lambda: v.tensor_tensor(grouped(b), grouped(b), wide(self.scale), ALU.mult),
            lambda: v.scalar_tensor_tensor(I(out), I(x), -0x80000000, I(b), ALU.bitwise_and, ALU.bitwise_or),
        )
        assert len(ops) == self.STEPS
        for k, op in enumerate(ops):
            if k:
                eng.wait_ge(sem, base + k)
            op().then_inc(sem, 1)


def quantise_weights(nc, ident, w_up, w_gate, w_down, up_t, gate_t, down_t, tag):
    with ExitStack() as ctx:
        sb, pm, sem = alloc(nc, ctx, tag)
        quant = {n: Fp4(nc, sb, f"q{n}", n) for n in (DIM, INNER)}
        jobs = []
        for w, dst in ((w_up, up_t), (w_gate, gate_t)):
            for m in range(IT):
                jobs.append((w, dst, m, 128 if m < IT - 1 else IREST, DIM))
        for m in range(HALVES):
            jobs.append((w_down, down_t, m, 128, INNER))
        rows = [sb(f"rows{s}", [128, INNER], F32) for s in range(2)]
        ps = [pm(f"ps{s}", [128, 8, 128], F32) for s in range(2)]
        filled = sem("filled")
        row_in = [sem(f"row_in{s}") for s in range(2)]
        steps, turned, copied = sem("steps"), sem("turned"), sem("copied")
        block = ctx.enter_context(nc.Block())

        @block.sync
        def _(sp):
            sp.wait_ge(filled, 2)
            for n, (w, dst, m, size, width) in enumerate(jobs):
                if n >= 2:
                    sp.wait_ge(turned, n - 1)
                sp.dma_start(rows[n % 2][0:size, 0:width], w[m * 128:m * 128 + size, :]).then_inc(row_in[n % 2], 16)

        @block.vector
        def _(dve):
            for s in range(2):
                nc.vector.memset(rows[s][:], 0.0).then_inc(filled, 1)
            for n, (w, dst, m, size, width) in enumerate(jobs):
                dve.wait_ge(row_in[n % 2], 16 * (n // 2 + 1))
                if n:
                    dve.wait_ge(steps, n * Fp4.STEPS)
                x = rows[n % 2][:, 0:width]
                quant[width].run(dve, steps, n * Fp4.STEPS, x, x)

        @block.tensor
        def _(pe):
            for n, (w, dst, m, size, width) in enumerate(jobs):
                pe.wait_ge(steps, (n + 1) * Fp4.STEPS)
                if n >= 2:
                    pe.wait_ge(copied, n - 1)
                for k in range(-(-width // 128)):
                    c = min(128, width - k * 128)
                    t = nc.tensor.transpose(ps[n % 2][0:c, k, 0:size], rows[n % 2][0:size, k * 128:k * 128 + c],
                                            ident[0:size, 0:size])
                t.then_inc(turned, 1)

        @block.scalar
        def _(act):
            for n, (w, dst, m, size, width) in enumerate(jobs):
                act.wait_ge(turned, n + 1)
                full = width // 128
                c = nc.scalar.copy(dst[:, 0:full, m * 128:m * 128 + size], ps[n % 2][:, 0:full, 0:size])
                if width % 128:
                    c = nc.scalar.copy(dst[0:width % 128, full, m * 128:m * 128 + size],
                                       ps[n % 2][0:width % 128, full, 0:size])
                c.then_inc(copied, 1)


def fp4_mlp(nc, resid, mean, rstd, ident, up_t, gate_t, down_t, out, tag):
    with ExitStack() as ctx:
        sb, pm, sem = alloc(nc, ctx, tag)
        HW = INNER // 2
        qx = Fp4(nc, sb, "qx", DIM)
        qh = Fp4(nc, sb, "qh", INNER)
        rows = [sb(f"rows{s}", [128, DIM], F32) for s in range(2)]
        rows_t = [sb(f"rows_t{s}", [128, HALVES, 128], F32) for s in range(2)]
        act_g = [sb(f"act_g{s}", [128, 2, HW], F32) for s in range(2)]
        hid = [sb(f"hid{s}", [128, INNER], F32) for s in range(2)]
        hid_t = [sb(f"hid_t{s}", [128, IT, 128], F32) for s in range(2)]
        done = [sb(f"done{s}", [128, DIM], F32) for s in range(2)]
        ps_t = pm("ps_t", [128, 8, 128], F32)
        ps_g = pm("ps_g", [128, 2, 512], F32)
        ps_u = pm("ps_u", [128, 2, 512], F32)
        ps_y = pm("ps_y", [128, DIM], F32)
        ps_x = pm("ps_x", [128, HALVES, 128], F32)
        xsteps, hsteps = sem("xsteps"), sem("hsteps")
        xturned, xcopied, scored, silu_done, multiplied, hturned, hcopied, projected, summed = (
            sem(n) for n in ("xturned", "xcopied", "scored", "silu_done", "multiplied", "hturned", "hcopied",
                             "projected", "summed"))
        stored = [sem(f"stored{s}") for s in range(2)]
        XS, HS = Fp4.STEPS + 1, Fp4.STEPS
        block = ctx.enter_context(nc.Block())

        def every_tile(eng, step):
            with eng.Fori(0, TILES // 2) as i:
                for s in range(2):
                    step(i, i * 2 + s, s)

        @block.vector
        def _(dve):
            def norm(i, t, s):
                dve.wait_ge(xturned, t)
                dve.wait_ge(xsteps, t * XS)
                nc.vector.tensor_scalar(rows[s][:], resid[:, bass.ds(t, 1), :].rearrange("p a d -> p (a d)"),
                                        mean[:, bass.ds(t, 1)], rstd[:, bass.ds(t, 1)], ALU.subtract, ALU.mult
                                        ).then_inc(xsteps, 1)
                dve.wait_ge(xsteps, t * XS + 1)
                qx.run(dve, xsteps, t * XS + 1, rows[s][:], rows[s][:])

            def hidden(i, t, s):
                dve.wait_ge(silu_done, t + 1)
                dve.wait_ge(hturned, t)
                dve.wait_ge(hsteps, t * HS)
                nc.vector.tensor_tensor(hid[s][:].rearrange("p (b c) -> p b c", b=2), ps_u[:, :, 0:HW], act_g[s][:], ALU.mult
                                        ).then_inc(multiplied, 1)
                dve.wait_ge(multiplied, t + 1)
                qh.run(dve, hsteps, t * HS, hid[s][:], hid[s][:])

            def finish(i, t, s):
                dve.wait_ge(projected, t + 1)
                dve.wait_ge(stored[s], i * 16)
                nc.vector.tensor_tensor(done[s][:], ps_y[:], resid[:, bass.ds(t, 1), :].rearrange("p a d -> p (a d)"),
                                        ALU.add).then_inc(summed, 1)

            def step(i, t, s, after=True):
                if after:
                    norm(i + s, t + 1, 1 - s)
                hidden(i, t, s)
                finish(i, t, s)

            norm(0, 0, 0)
            with dve.Fori(0, TILES // 2 - 1) as i:
                for s in range(2):
                    step(i, i * 2 + s, s)
            last = TILES // 2 - 1
            step(last, TILES - 2, 0)
            step(last, TILES - 1, 1, False)

        @block.tensor
        def _(pe):
            def turn_x(i, t, s):
                pe.wait_ge(xsteps, t * XS + XS)
                pe.wait_ge(xcopied, t)
                for f in range(HALVES):
                    m = nc.tensor.transpose(ps_x[:, f, :], rows[s][:, f * 128:(f + 1) * 128], ident[:])
                m.then_inc(xturned, 1)

            def score(i, t, s):
                pe.wait_ge(xcopied, t + 1)
                pe.wait_ge(multiplied, t)
                for ps, w in ((ps_g, gate_t), (ps_u, up_t)):
                    for h in range(2):
                        for k in range(HALVES):
                            m = nc.tensor.matmul(ps[:, h, 0:HW], rows_t[s][:, k, :], w[:, k, h * HW:(h + 1) * HW],
                                                 start=k == 0, stop=k == HALVES - 1)
                m.then_inc(scored, 1)

            def down(i, t, s):
                pe.wait_ge(hsteps, t * HS + HS)
                pe.wait_ge(hcopied, t)
                for k in range(IT):
                    c = 128 if k < IT - 1 else IREST
                    m = nc.tensor.transpose(ps_t[0:c, k, :], hid[s][:, k * 128:k * 128 + c], ident[:])
                m.then_inc(hturned, 1)
                pe.wait_ge(hcopied, t + 1)
                pe.wait_ge(summed, t)
                for k in range(IT):
                    c = 128 if k < IT - 1 else IREST
                    m = nc.tensor.matmul(ps_y[:], hid_t[s][0:c, k, :], down_t[0:c, k, :], start=k == 0, stop=k == IT - 1)
                m.then_inc(projected, 1)

            def step(i, t, s, after=True):
                if after:
                    turn_x(i + s, t + 1, 1 - s)
                down(i, t, s)
                if after:
                    score(i + s, t + 1, 1 - s)

            turn_x(0, 0, 0)
            score(0, 0, 0)
            with pe.Fori(0, TILES // 2 - 1) as i:
                for s in range(2):
                    step(i, i * 2 + s, s)
            last = TILES // 2 - 1
            step(last, TILES - 2, 0)
            step(last, TILES - 1, 1, False)

        @block.scalar
        def _(act):
            def copy_x(i, t, s):
                act.wait_ge(xturned, t + 1)
                nc.scalar.copy(rows_t[s][:], ps_x[:]).then_inc(xcopied, 1)

            def silu(i, t, s):
                act.wait_ge(scored, t + 1)
                nc.scalar.activation(act_g[s][:], ps_g[:, :, 0:HW], ACT.Silu).then_inc(silu_done, 1)

            def copy_h(i, t, s):
                act.wait_ge(hturned, t + 1)
                nc.scalar.copy(hid_t[s][:, 0:IT - 1, :], ps_t[:, 0:IT - 1, :])
                nc.scalar.copy(hid_t[s][0:IREST, IT - 1, :], ps_t[0:IREST, IT - 1, :]).then_inc(hcopied, 1)

            def step(i, t, s, after=True):
                if after:
                    copy_x(i + s, t + 1, 1 - s)
                copy_h(i, t, s)
                if after:
                    silu(i + s, t + 1, 1 - s)

            copy_x(0, 0, 0)
            silu(0, 0, 0)
            with act.Fori(0, TILES // 2 - 1) as i:
                for s in range(2):
                    step(i, i * 2 + s, s)
            last = TILES // 2 - 1
            step(last, TILES - 2, 0)
            step(last, TILES - 1, 1, False)

        @block.sync
        def _(sp):
            view = out.rearrange("(t p) d -> p t d", p=128)

            def step(i, t, s):
                sp.wait_ge(summed, t + 1)
                sp.dma_start(view[:, bass.ds(t, 1), :].rearrange("p a d -> p (a d)"), done[s][:]).then_inc(stored[s], 16)

            every_tile(sp, step)
            for s in range(2):
                sp.wait_ge(stored[s], 16 * (TILES // 2))


def ffn_layer(nc, resid, ident, a, out, tag):
    with ExitStack() as ctx:
        sb, _, _ = alloc(nc, ctx, tag)
        mean, rstd = sb("mean", [128, TILES], F32), sb("rstd", [128, TILES], F32)
        up_t = sb("up_t", [128, HALVES, INNER], F32)
        gate_t = sb("gate_t", [128, HALVES, INNER], F32)
        down_t = sb("down_t", [128, IT, DIM], F32)
        norm_stats(nc, resid, mean, rstd, tag + "n")
        quantise_weights(nc, ident, a["w_up"], a["w_gate"], a["w_down"], up_t, gate_t, down_t, tag + "q")
        fp4_mlp(nc, resid, mean, rstd, ident, up_t, gate_t, down_t, out, tag + "m")


def tower(nc, a, out):
    with ExitStack() as ctx:
        resid = ctx.enter_context(nc.sbuf_tensor("resid", [128, TILES, DIM], F32))
        ident = ctx.enter_context(nc.sbuf_tensor("ident", [128, 128], F32))
        make_identity(nc, ident, "id")
        embed(nc, a["ids"], [a["emb0"], a["emb1"], a["emb2"]], [a["w0"], a["w1"], a["w2"]],
              [a["b0"], a["b1"], a["b2"]], resid, ident, "e")
        attention_layer(nc, resid, ident, {k: a["a0_" + k] for k in ("q", "k", "v", "latent", "bq", "bk", "bl", "bv")},
                        a["a0_out"], a["a0_bo"], None, float(HEAD_DIM) ** -0.5, "A")
        moe_layer(nc, resid, ident, a, "M")
        attention_layer(nc, resid, ident, {k: a["a1_" + k] for k in ("q", "k", "v")},
                        a["a1_out"], a["a1_bo"], a["alibi"], float(HEAD_DIM) ** 0.5, "B")
        ffn_layer(nc, resid, ident, a, out, "F")


def kernel(**inputs):
    import concourse.bacc as bacc
    from concourse.bass_utils import run_bass_kernel_spmd

    z = {k: np.asarray(v) for k, v in inputs.items()}
    C = np.ascontiguousarray
    arrays = {"ids": C(z["x"].reshape(TILES, 128).T)}
    for k in range(3):
        arrays[f"emb{k}"] = C(z[f"L0_tok_emb{k}"])
        arrays[f"w{k}"] = C(z[f"L0_tok_w{k}"].T)
        arrays[f"b{k}"] = C(z[f"L0_tok_b{k}"].reshape(1, DIM))
    for name, key in (("q", "Wq"), ("k", "Wk"), ("v", "Wv"), ("latent", "Wl"), ("bl", "bl"), ("bv", "bv"),
                      ("out", "Wo"), ("bo", "bo")):
        arrays["a0_" + name] = C(z["L0_attn_" + key])
    for name in ("bq", "bk"):
        arrays["a0_" + name] = C(z["L0_attn_" + name].reshape(HALVES, 128))
    for name, key in (("q", "Wq"), ("k", "Wk"), ("v", "Wv"), ("out", "Wp")):
        arrays["a1_" + name] = C(z["L1_attn_" + key].T)
    arrays["a1_bo"] = C(z["L1_attn_bp"])
    arrays["alibi"] = alibi_rows()
    arrays.update(moe_arrays(z))
    for name in ("w_gate", "w_up", "w_down"):
        arrays[name] = C(z["L1_ffn_" + name])

    nc = bacc.Bacc("TRN2", target_bir_lowering=False, num_devices=1)
    a = {k: nc.dram_tensor(f"in_{k}", v.shape, mybir.dt.from_np(v.dtype), kind="ExternalInput").ap()
         for k, v in arrays.items()}
    out = nc.dram_tensor("out", (TOKENS, DIM), F32, kind="ExternalOutput").ap()
    tower(nc, a, out)
    result = run_bass_kernel_spmd(nc, [{f"in_{k}": v for k, v in arrays.items()}], core_ids=[0])
    return result.results[0]["out"].reshape(BATCH, SEQ, DIM)
```

```python
from contextlib import ExitStack

import numpy as np

import concourse.bass as bass
from concourse import mybir

F32 = mybir.dt.float32
BF16 = mybir.dt.bfloat16
I32 = mybir.dt.int32
ALU = mybir.AluOpType
ACT = mybir.ActivationFunctionType
AX = mybir.AxisListType

BATCH, SEQ, DIM = 2, 2048, 256
HEADS, HEAD_DIM = 16, 16
PAIRS = BATCH * HEADS
TOKENS = BATCH * SEQ
TILES = TOKENS // 128
HALVES = DIM // 128
CHUNK = 4
EPS = 1e-5
LATENT = DIM // 4

CUTOFFS = (0, 5000, 10000, 50258)
EMB_DIMS = (256, 64, 16)
CAT = sum(EMB_DIMS) + 3

EXPERTS, FFN = 8, 816
FT = -(-FFN // 128)
FREST = FFN - (FT - 1) * 128
BLOCK = 256
BLOCKS = (2 * TOKENS + EXPERTS * (BLOCK - 1)) // BLOCK
SUBS = BLOCK // 128
UP, GATE, DOWN, UPB, GATEB = 0, 2 * FFN, 4 * FFN, 4 * FFN + FT * DIM, 4 * FFN + FT * DIM + FT
EROW = GATEB + FT

INNER = 704
QUANT = 16
IT = -(-INNER // 128)
IREST = INNER - (IT - 1) * 128


class Chain:

    def __init__(self, eng, sem):
        self.eng, self.sem, self.n = eng, sem, 0

    def step(self, ins):
        ins.then_inc(self.sem, 1)
        self.n += 1
        self.eng.wait_ge(self.sem, self.n)


class Head:

    def __init__(self, turn, c):
        self.turn, self.c = turn, c
        self.n = turn * 4 + c
        self.slot = c % 4
        self.fills = turn + (c // 4 + 1)
        self.first = isinstance(turn, int) and c == 0

    def ahead(self, k):
        return Head(self.turn, self.c + k)

    def at_least(self, k):
        return not isinstance(self.turn, int) or self.c >= k


def attention_core(nc, parts_q, parts_k, values, attended, bias_rows, scale, heads, tag):
    with ExitStack() as ctx:
        sb, pm, sem = alloc(nc, ctx, tag)

        KT = SEQ // 128
        QB = SEQ // 512
        NB = QB * KT
        NA = KT * QB
        GROUP = 4
        NG = NB // GROUP
        AHEAD = 16
        KD = 6 * HEAD_DIM
        KS = KD + (6 if bias_rows else 0)
        KM = KS + 3
        LOADS = 6 + (2 if bias_rows else 0)

        q_rows = [sb(f"q_rows{s}", [128, SEQ], BF16) for s in range(4)]
        k_rows = [sb(f"k_rows{s}", [128, SEQ], BF16) for s in range(4)]
        v_ones = [sb(f"v_ones{s}", [128, KT, 32], F32) for s in range(4)]
        probs = [sb(f"probs{s}", [128, 512], F32) for s in range(8)]
        out_t = sb("out_t", [128, SEQ], F32)
        fold = sb("fold", [128, 17], F32)
        fold_i = sb("fold_i", [128, 17], F32)
        ident = sb("ident", [128, 128], BF16)
        tile_max = sb("tile_max", [128, 2, KT, QB], F32)
        row_max = sb("row_max", [128, KT], F32)
        rest = sb("rest", [128, KT], F32)
        rest2 = sb("rest2", [128, KT], F32)
        max_parts = sb("max_parts", [128, 128], BF16)
        max_rows = [sb(f"max_rows{s}", [3 * KT, 128], BF16) for s in range(2)]
        inv = sb("inv", [128, KT], F32)

        ps_max = [pm(f"ps_max{s}", [128, 512], F32) for s in range(3)]
        ps_s = [pm(f"ps_s{s}", [128, 512], F32) for s in range(3)]
        ps_o = pm("ps_o", [128, 512], F32)
        ps_x = pm("ps_x", [128, 512], F32)
        ps_maxt = ps_x[:, 448:512].bitcast(BF16)

        const_ready = sem("const_ready")
        ones_ready = sem("ones_ready")
        loaded = [sem(f"loaded{s}") for s in range(4)]
        max_in_place = [sem(f"max_in_place{s}") for s in range(4)]
        v_filled = sem("v_filled")
        v_ready = sem("v_ready")
        tile_scored = sem("tile_scored")
        tile_reduced = sem("tile_reduced")
        split_step = sem("split_step")
        max_turned = sem("max_turned")
        max_copied = sem("max_copied")
        scored = sem("scored")
        exp_done = sem("exp_done")
        pv_done = sem("pv_done")
        out_copied = sem("out_copied")
        folded = sem("folded")
        inverted = sem("inverted")
        normed = sem("normed")
        fold_step = sem("fold_step")
        SPLITS = 6

        block = ctx.enter_context(nc.Block())

        LOOPS = (heads - 4) // 4
        assert LOOPS * 4 == heads - 4

        def every_head(eng, step):
            step(Head(0, 0), 3)
            with eng.Fori(0, LOOPS) as i:
                for u in range(1, 5):
                    step(Head(i, u), 3)
            for c in range(heads - 3, heads):
                step(Head(0, c), heads - 1 - c)

        @block.sync
        def _(sp):
            def load(h):
                q, k = q_rows[h.slot], k_rows[h.slot]
                for part, copies, at in ((0, 3, 0), (1, 2, 3), (2, 1, 5)):
                    a, b = at * HEAD_DIM, (at + copies) * HEAD_DIM
                    sp.dma_start(q[a:b, :], parts_q[part, bass.ds(h.n, 1), :, :].to_broadcast(
                        [copies, HEAD_DIM, SEQ])).then_inc(loaded[h.slot], 16)
                    sp.dma_start(k[a:b, :], parts_k[0:copies, bass.ds(h.n, 1), :, :].rearrange("c a d n -> c (a d) n")
                                 ).then_inc(loaded[h.slot], 16)
                if bias_rows:
                    for rows, table in ((q, bias_rows[0]), (k, bias_rows[1])):
                        sp.dma_start(rows[KD:KS, :], table[bass.ds(h.n, 1), :, :].rearrange("a d n -> (a d) n")
                                     ).then_inc(loaded[h.slot], 16)

            sp.wait_ge(ones_ready, 4)
            for s in range(3):
                load(Head(0, s))

            def place_max(h):
                sp.wait_ge(max_copied, h.n + 1)
                for part in range(3):
                    sp.dma_start(q_rows[h.slot][KS + part:KS + part + 1, :].rearrange("a (t n) -> a t n", n=128),
                                 max_rows[h.slot % 2][part * KT:(part + 1) * KT, :]).then_inc(max_in_place[h.slot], 16)

            def step(h, after):
                place_max(h)
                if after >= 3:
                    sp.wait_ge(scored, h.n * NB)
                    load(h.ahead(3))

            every_head(sp, step)

        @block.gpsimd
        def _(pool):
            nc.gpsimd.iota(fold_i[:], pattern=[[-1, 17]], base=128, channel_multiplier=1,
                           allow_small_or_imprecise_dtypes=True).then_inc(const_ready, 1)
            nc.gpsimd.memset(ident[:], 0.0).then_inc(const_ready, 1)
            pool.wait_ge(const_ready, 2)
            nc.gpsimd.affine_select(out=ident[:], in_=ident[:], compare_op=ALU.not_equal, fill=1.0, base=0,
                                    pattern=[[-1, 128]], channel_multiplier=1).then_inc(const_ready, 1)
            pool.wait_ge(v_filled, 8)

            def fetch_v(h):
                nc.gpsimd.tensor_copy(v_ones[h.slot][:, :, 0:HEAD_DIM],
                                      values[:, bass.ds(h.n, 1), :, :].rearrange("p a t d -> p (a t) d")).then_inc(v_ready, 1)

            for s in range(3):
                fetch_v(Head(0, s))

            def step(h, after):
                if after >= 3:
                    pool.wait_ge(pv_done, h.n * NG + 1)
                    fetch_v(h.ahead(3))

            every_head(pool, step)

        def tiles_of_step(after):
            out = []
            for k in range(NA):
                ahead, n = (1, k + AHEAD) if k + AHEAD < NA else (2, k + AHEAD - NA)
                out.append((ahead, n) if ahead <= after else None)
            return out

        @block.tensor
        def _(pe):
            def score_for_max(h, n):
                if n == 0:
                    pe.wait_ge(loaded[h.slot], h.fills * 16 * LOADS)
                if h.at_least(1) or n >= 3:
                    pe.wait_ge(tile_reduced, h.n * NA + max(n - 2, 0))
                qt, kb = n // QB, n % QB
                nc.tensor.matmul(ps_max[n % 3][:], q_rows[h.slot][0:KS, qt * 128:(qt + 1) * 128],
                                 k_rows[h.slot][0:KS, kb * 512:(kb + 1) * 512], start=True, stop=True
                                 ).then_inc(tile_scored, 1)

            def turn_max(h):
                pe.wait_ge(split_step, SPLITS * (h.n + 1))
                if h.at_least(2):
                    pe.wait_ge(normed, h.n)
                nc.tensor.transpose(ps_maxt[:, 0:128], max_parts[:],
                                    ident[:]).then_inc(max_turned, 1)

            def score(h, n):
                if n == 0:
                    pe.wait_ge(max_in_place[h.slot], 48 * h.fills)
                if h.at_least(1) or n >= 3:
                    pe.wait_ge(exp_done, h.n * NB + max(n - 2, 0))
                qb, kt = n // KT, n % KT
                nc.tensor.matmul(ps_s[n % 3][:], k_rows[h.slot][0:KM, kt * 128:(kt + 1) * 128],
                                 q_rows[h.slot][0:KM, qb * 512:(qb + 1) * 512], start=True, stop=True).then_inc(scored, 1)

            def times_v(h, j):
                per = KT // GROUP
                if j == 0:
                    pe.wait_ge(v_ready, h.n + 1)
                if j % per == 0:
                    pe.wait_ge(out_copied, h.n * QB + j // per)
                pe.wait_ge(exp_done, h.n * NB + (j + 1) * GROUP)
                for c in range(GROUP):
                    kt = (j % per) * GROUP + c
                    m = nc.tensor.matmul(ps_o[32 * c:32 * c + 32, :], v_ones[h.slot][:, kt, :],
                                         probs[(j % 2) * GROUP + c][:], start=(j % per == 0), stop=(j % per == per - 1))
                m.then_inc(pv_done, 1)

            def fold_out(h, after):
                pe.wait_ge(out_copied, (h.n + 1) * QB)
                pe.wait_ge(normed, h.n + 1)
                pe.wait_ge(max_copied, h.n + 1 + (1 if after else 0))
                for t in range(KT):
                    m = nc.tensor.matmul(ps_x[:, t * 17:(t + 1) * 17], out_t[:, t * 128:(t + 1) * 128], fold[:],
                                         start=True, stop=True)
                m.then_inc(folded, 1)

            nc.tensor.nop().then_inc(pv_done, 1)
            pe.wait_ge(const_ready, 4)
            pe.wait_ge(ones_ready, 4)
            for n in range(NA):
                score_for_max(Head(0, 0), n)
            for n in range(AHEAD):
                score_for_max(Head(0, 1), n)
            turn_max(Head(0, 0))

            def step(h, after):
                tiles = tiles_of_step(after)
                turn_at = NA - AHEAD + 3
                for n in range(NB):
                    score(h, n)
                    if n == 2 and not h.first:
                        times_v(h.ahead(-1), NG - 1)
                    if n == 12 and not h.first:
                        fold_out(h.ahead(-1), True)
                    if tiles[n]:
                        ahead, k = tiles[n]
                        score_for_max(h.ahead(ahead), k)
                    if n % 4 == 3 and n > 4:
                        times_v(h, n // 4 - 1)
                    if n == turn_at and after:
                        turn_max(h.ahead(1))

            every_head(pe, step)
            times_v(Head(0, heads - 1), NG - 1)
            fold_out(Head(0, heads - 1), False)

        @block.scalar
        def _(act):
            def exps(h, n):
                act.wait_ge(scored, h.n * NB + n + 1)
                if n % GROUP == 0:
                    act.wait_ge(pv_done, h.n * NG + n // GROUP)
                nc.scalar.activation(probs[n % 8][:], ps_s[n % 3][:], ACT.Exp, scale=scale).then_inc(exp_done, 1)

            def copy_out(h, qb):
                act.wait_ge(pv_done, h.n * NG + (qb + 1) * (NG // QB) + 1)
                if qb == 0:
                    act.wait_ge(folded, h.n)
                nc.scalar.copy(out_t[:, qb * 512:(qb + 1) * 512], ps_o[:]).then_inc(out_copied, 1)

            def copy_max(h):
                act.wait_ge(max_turned, h.n + 1)
                if h.at_least(2):
                    act.wait_ge(max_in_place[h.ahead(-2).slot], 48 * h.ahead(-2).fills)
                nc.scalar.copy(max_rows[h.slot % 2][:], ps_maxt[0:3 * KT, 0:128]).then_inc(max_copied, 1)

            copy_max(Head(0, 0))

            def step(h, after):
                for n in range(NB):
                    exps(h, n)
                    if n == 6 and not h.first:
                        copy_out(h.ahead(-1), QB - 1)
                    if n % KT == 5 and n > KT:
                        copy_out(h, n // KT - 1)
                    if n == NA - AHEAD + 5 and after:
                        copy_max(h.ahead(1))

            every_head(act, step)
            copy_out(Head(0, heads - 1), QB - 1)

        @block.vector
        def _(dve):
            def reduce_tile(h, n):
                dve.wait_ge(tile_scored, h.n * NA + n + 1)
                nc.vector.tensor_reduce(tile_max[:, h.slot % 2, n // QB, n % QB:n % QB + 1], ps_max[n % 3][:], AX.X, ALU.max
                                        ).then_inc(tile_reduced, 1)

            def split_max(h):
                dve.wait_ge(tile_reduced, (h.n + 1) * NA)
                if h.at_least(1):
                    dve.wait_ge(max_turned, h.n)
                tiles = tile_max[:, h.slot % 2, :, :]
                ops = [
                    lambda: nc.vector.tensor_reduce(row_max[:], tiles, AX.X, ALU.max, negate=True),
                    lambda: nc.vector.tensor_copy(max_parts[:, 0 * KT:1 * KT], row_max[:]),
                    lambda: nc.vector.tensor_tensor(rest[:], row_max[:], max_parts[:, 0 * KT:1 * KT], ALU.subtract),
                    lambda: nc.vector.tensor_copy(max_parts[:, 1 * KT:2 * KT], rest[:]),
                    lambda: nc.vector.tensor_tensor(rest2[:], rest[:], max_parts[:, 1 * KT:2 * KT], ALU.subtract),
                    lambda: nc.vector.tensor_copy(max_parts[:, 2 * KT:3 * KT], rest2[:]),
                ]
                for n, op in enumerate(ops):
                    if n:
                        dve.wait_ge(split_step, h.n * SPLITS + n)
                    op().then_inc(split_step, 1)

            def norm(h):
                dve.wait_ge(folded, h.n + 1)
                turned = ps_x[:, 0:17 * KT].rearrange("p (t d) -> p t d", d=17)
                nc.vector.reciprocal(inv[:], turned[:, :, 16]).then_inc(inverted, 1)
                dve.wait_ge(inverted, h.n + 1)
                nc.vector.tensor_tensor(attended[:, bass.ds(h.n, 1), :, :].rearrange("p a t d -> p (a t) d"),
                                        turned[:, :, 0:HEAD_DIM], inv[:].unsqueeze(2).to_broadcast([128, KT, HEAD_DIM]),
                                        ALU.mult).then_inc(normed, 1)

            nc.vector.nop().then_inc(normed, 1)
            nc.vector.memset(max_parts[:], 0.0).then_inc(fold_step, 1)
            for s in range(4):
                nc.vector.memset(k_rows[s][96:128, :], 1.0).then_inc(ones_ready, 1)
            for s in range(4):
                nc.vector.memset(v_ones[s][:, :, 16:17], 1.0).then_inc(v_filled, 1)
                nc.vector.memset(v_ones[s][:, :, 17:32], 0.0).then_inc(v_filled, 1)
            dve.wait_ge(const_ready, 3)
            nc.vector.tensor_scalar(fold[:], fold_i[:], 128.0, None, ALU.is_equal).then_inc(fold_step, 1)
            for k in range(1, 4):
                dve.wait_ge(fold_step, k + 1)
                nc.vector.scalar_tensor_tensor(fold[:], fold_i[:], 128.0 + 32 * k, fold[:], ALU.is_equal, ALU.add
                                               ).then_inc(const_ready if k == 3 else fold_step, 1)
            for n in range(NA):
                reduce_tile(Head(0, 0), n)
            split_max(Head(0, 0))
            for n in range(AHEAD):
                reduce_tile(Head(0, 1), n)

            def step(h, after):
                for k, tile in enumerate(tiles_of_step(after)):
                    if tile:
                        ahead, n = tile
                        reduce_tile(h.ahead(ahead), n)
                    if k == NA - AHEAD - 1 and after:
                        split_max(h.ahead(1))
                    if k == 18 and not h.first:
                        norm(h.ahead(-1))

            every_head(dve, step)
            norm(Head(0, heads - 1))


def alloc(nc, ctx, tag):
    sems = []

    @ctx.callback
    def _():
        if sems:
            nc.clear_and_free_semaphores(sems)
            nc.all_engine_barrier()

    def sem(n, lasting=False):
        s = nc.alloc_semaphore(f"{tag}_{n}")
        if not lasting:
            sems.append(s)
        return s

    return (lambda n, s, d: ctx.enter_context(nc.sbuf_tensor(f"{tag}_{n}", s, d)),
            lambda n, s, d: ctx.enter_context(nc.psum_tensor(f"{tag}_{n}", s, d)), sem)


def make_identity(nc, ident, tag):
    with ExitStack() as ctx:
        _, _, sem = alloc(nc, ctx, tag)
        zeroed, made = sem("zeroed"), sem("made")
        block = ctx.enter_context(nc.Block())

        @block.gpsimd
        def _(pool):
            nc.gpsimd.memset(ident[:], 0.0).then_inc(zeroed, 1)
            pool.wait_ge(zeroed, 1)
            nc.gpsimd.affine_select(out=ident[:], in_=ident[:], compare_op=ALU.not_equal, fill=1.0, base=0,
                                    pattern=[[-1, 128]], channel_multiplier=1).then_inc(made, 1)
            pool.wait_ge(made, 1)


def embed(nc, ids, tables, weights, biases, resid, ident, tag):
    with ExitStack() as ctx:
        sb, pm, sem = alloc(nc, ctx, tag)
        ids_i = sb("ids_i", [128, TILES], I32)
        ids_f = sb("ids_f", [128, TILES], F32)
        low = sb("low", [128, TILES], F32)
        index_f = sb("index_f", [128, TILES], F32)
        index = sb("index", [128, TILES, 3], I32)
        mask = sb("mask", [128, 3, TILES], F32)
        proj = sb("proj", [128, 3, DIM], F32)
        at_hand = [sb(f"at_hand{s}", [128, 3], I32) for s in range(2)]
        rows = [sb(f"rows{s}", [128, sum(EMB_DIMS)], F32) for s in range(2)]
        cat = [sb(f"cat{s}", [128, 384], F32) for s in range(2)]
        cat_t = [sb(f"cat_t{s}", [128, 3, 128], F32) for s in range(2)]
        ps_t = [pm(f"ps_t{s}", [128, 3, 128], F32) for s in range(2)]
        ps_e = [pm(f"ps_e{s}", [128, DIM], F32) for s in range(2)]
        ids_in, w_in = sem("ids_in"), sem("w_in")
        prep = sem("prep")
        gathered = [sem(f"gathered{s}", lasting=True) for s in range(2)]
        masked, masks, turned, copied, projected, stored = (
            sem(n) for n in ("masked", "masks", "turned", "copied", "projected", "stored"))
        PREP = 16
        block = ctx.enter_context(nc.Block())

        @block.sync
        def _(sp):
            sp.dma_start(ids_i[:], ids).then_inc(ids_in, 16)
            for k in range(HALVES):
                sp.dma_start(proj[:, k, :], weights[0][k * 128:(k + 1) * 128, :]).then_inc(w_in, 16)
            d1, d2 = EMB_DIMS[1], EMB_DIMS[2]
            sp.dma_start(proj[0:d1, 2, :], weights[1]).then_inc(w_in, 16)
            sp.dma_start(proj[d1:d1 + d2, 2, :], weights[2]).then_inc(w_in, 16)
            for k in range(3):
                sp.dma_start(proj[d1 + d2 + k:d1 + d2 + k + 1, 2, :], biases[k]).then_inc(w_in, 16)

        @block.vector
        def _(dve):
            dve.wait_ge(ids_in, 16)
            chain = Chain(dve, prep)
            chain.step(nc.vector.tensor_copy(ids_f[:], ids_i[:]))
            for k in range(3):
                lo, hi = CUTOFFS[k], CUTOFFS[k + 1]
                chain.step(nc.vector.tensor_scalar(low[:], ids_f[:], float(lo), None, ALU.is_ge))
                chain.step(nc.vector.scalar_tensor_tensor(mask[:, k, :], ids_f[:], float(hi), low[:], ALU.is_lt, ALU.mult))
                chain.step(nc.vector.tensor_scalar(index_f[:], ids_f[:], float(-lo), 0.0, ALU.add, ALU.max))
                chain.step(nc.vector.tensor_scalar(index[:, :, k], index_f[:], float(hi - lo - 1), None, ALU.min))
            for s in range(2):
                chain.step(nc.vector.memset(cat[s][:], 0.0))
            nc.vector.nop().then_inc(prep, PREP - chain.n)

            with dve.Fori(0, TILES // 2) as i:
                for s in range(2):
                    t = i * 2 + s
                    dve.wait_ge(gathered[s], i * 48 + 48)
                    dve.wait_ge(turned, t)
                    at = 0
                    for k, d in enumerate(EMB_DIMS):
                        nc.vector.tensor_scalar(cat[s][:, at:at + d], rows[s][:, at:at + d], mask[:, k, bass.ds(t, 1)],
                                                None, ALU.mult).then_inc(masked, 1)
                        at += d
                    nc.vector.tensor_copy(cat[s][:, at:at + 3], mask[:, :, bass.ds(t, 1)].rearrange("p k a -> p (k a)")
                                          ).then_inc(masked, 1)

        @block.gpsimd
        def _(pool):
            pool.wait_ge(prep, PREP)
            with pool.Fori(0, TILES // 2) as i:
                for s in range(2):
                    t = i * 2 + s
                    pool.wait_ge(masked, t * 4 + 4)
                    nc.gpsimd.tensor_copy(at_hand[s][:], index[:, bass.ds(t, 1), :].rearrange("p a k -> p (a k)")
                                          )
                    pool.drain()
                    at = 0
                    for k, d in enumerate(EMB_DIMS):
                        nc.gpsimd.indirect_dma_start(
                            rows[s][:, at:at + d], None, tables[k],
                            bass.IndirectOffsetOnAxis(ap=at_hand[s][:, k:k + 1], axis=0)).then_inc(gathered[s], 16)
                        at += d

        @block.tensor
        def _(pe):
            pe.wait_ge(w_in, 16 * (HALVES + 5))
            with pe.Fori(0, TILES // 2) as i:
                for s in range(2):
                    t = i * 2 + s
                    pe.wait_ge(masked, t * 4 + 4 + 8)
                    pe.wait_ge(copied, t)
                    for k in range(3):
                        m = nc.tensor.transpose(ps_t[s][:, k, :], cat[s][:, k * 128:(k + 1) * 128], ident[:])
                    m.then_inc(turned, 1)
                    pe.wait_ge(copied, t + 1)
                    pe.wait_ge(stored, t)
                    for k in range(3):
                        n = 128 if k < 2 else CAT - 256
                        m = nc.tensor.matmul(ps_e[s][:], cat_t[s][0:n, k, :], proj[0:n, k, :], start=k == 0, stop=k == 2)
                    m.then_inc(projected, 1)

        @block.scalar
        def _(act):
            nc.scalar.nop().then_inc(masked, 8)
            with act.Fori(0, TILES // 2) as i:
                for s in range(2):
                    t = i * 2 + s
                    act.wait_ge(turned, t + 1)
                    nc.scalar.copy(cat_t[s][:], ps_t[s][:]).then_inc(copied, 1)
                    act.wait_ge(projected, t + 1)
                    nc.scalar.mul(resid[:, bass.ds(t, 1), :].rearrange("p a d -> p (a d)"), ps_e[s][:], float(DIM) ** 0.5
                                  ).then_inc(stored, 1)


def norm_stats(nc, resid, mean, rstd, tag):
    with ExitStack() as ctx:
        sb, _, sem = alloc(nc, ctx, tag)
        stats = sb("stats", [128, TILES, 6], F32)
        a, b, var, root, inv = (sb(n, [128, TILES], F32) for n in ("a", "b", "var", "root", "inv"))
        rows_done, chained, root_done = sem("rows_done"), sem("chained"), sem("root_done")
        block = ctx.enter_context(nc.Block())

        @block.vector
        def _(dve):
            for t in range(TILES):
                nc.vector.bn_stats(stats[:, t, :], resid[:, t, :]).then_inc(rows_done, 1)
            dve.wait_ge(rows_done, TILES)
            chain = Chain(dve, chained)
            m0, v0, m1, v1 = (stats[:, :, k] for k in (1, 2, 4, 5))
            chain.step(nc.vector.tensor_tensor(a[:], m0, m1, ALU.subtract))
            chain.step(nc.vector.tensor_tensor(a[:], a[:], a[:], ALU.mult))
            chain.step(nc.vector.tensor_tensor(b[:], v0, v1, ALU.add))
            chain.step(nc.vector.tensor_scalar(b[:], b[:], 1.0 / DIM, EPS, ALU.mult, ALU.add))
            chain.step(nc.vector.scalar_tensor_tensor(var[:], a[:], 0.25, b[:], ALU.mult, ALU.add))
            chain.step(nc.vector.tensor_tensor(b[:], m0, m1, ALU.add))
            chain.step(nc.vector.tensor_scalar(mean[:], b[:], 0.5, None, ALU.mult))
            dve.wait_ge(root_done, 1)
            chain.step(nc.vector.reciprocal(inv[:], root[:]))
            chain.step(nc.vector.tensor_tensor(a[:], inv[:], inv[:], ALU.mult))
            chain.step(nc.vector.tensor_tensor(a[:], a[:], var[:], ALU.mult))
            chain.step(nc.vector.tensor_scalar(a[:], a[:], -0.5, 1.5, ALU.mult, ALU.add))
            chain.step(nc.vector.tensor_tensor(rstd[:], inv[:], a[:], ALU.mult))

        @block.scalar
        def _(act):
            act.wait_ge(chained, 5)
            nc.scalar.activation(root[:], var[:], ACT.Sqrt).then_inc(root_done, 1)


def project_qkv(nc, resid, mean, rstd, ident, parts_q, parts_k, values, w, tag):
    latent = "latent" in w
    with ExitStack() as ctx:
        sb, pm, sem = alloc(nc, ctx, tag)
        KD = LATENT if latent else 128
        KN = 1 if latent else HALVES
        wq = sb("wq", [128, HALVES, DIM], F32)
        wk = sb("wk", [KD, KN, DIM], F32)
        wv = sb("wv", [KD, KN, DIM], F32)
        if latent:
            wl = sb("wl", [128, HALVES, LATENT], F32)
            bias_qk = sb("bias_qk", [128, 2, HALVES], F32)
            bias_l = sb("bias_l", [LATENT, 1], F32)
            bias_v = sb("bias_v", [1, DIM], F32)
            ones = sb("ones", [1, 128], F32)
            lat = sb("lat", [LATENT, 512], F32)
        rows = sb("rows", [128, CHUNK, DIM], F32)
        rows_t = sb("rows_t", [128, HALVES, 512], F32)
        whole = [sb(f"whole{n}", [128, HALVES, 512], F32) for n in "qk"]
        rest = [sb(f"rest{n}", [128, HALVES, 512], F32) for n in "qk"]
        parts = [sb(f"parts{n}", [128, 3, HALVES, 512], BF16) for n in "qk"]
        ps_t = pm("ps_t", [128, HALVES, 512], F32)
        ps_qk = [pm(f"ps_{n}", [128, HALVES, 512], F32) for n in "qk"]
        ps_v = pm("ps_v", [128, CHUNK, DIM], F32)
        w_in, ones_set = sem("w_in"), sem("ones_set")
        normed, turned, copied, lat_done, lat_copied, v_done, v_stored = (
            sem(n) for n in ("normed", "turned", "copied", "lat_done", "lat_copied", "v_done", "v_stored"))
        done = [sem(f"{n}_done") for n in "qk"]
        out = [sem(f"{n}_out") for n in "qk"]
        split = [sem(f"{n}_split") for n in "qk"]
        stored = [sem(f"{n}_stored") for n in "qk"]
        CH = TILES // CHUNK // BATCH
        loads = []
        for k in range(HALVES):
            loads.append((wq[:, k, :], w["q"][k * 128:(k + 1) * 128, :]))
        for k in range(KN):
            loads.append((wk[:, k, :], w["k"][k * KD:(k + 1) * KD, :]))
            loads.append((wv[:, k, :], w["v"][k * KD:(k + 1) * KD, :]))
        if latent:
            for k in range(HALVES):
                loads.append((wl[:, k, :], w["latent"][k * 128:(k + 1) * 128, :]))
                loads.append((bias_qk[:, 0, k:k + 1], w["bq"][k].unsqueeze(1)))
                loads.append((bias_qk[:, 1, k:k + 1], w["bk"][k].unsqueeze(1)))
            loads.append((bias_l[:], w["bl"].unsqueeze(1)))
            loads.append((bias_v[:], w["bv"].unsqueeze(0)))
        block = ctx.enter_context(nc.Block())

        def every_chunk(eng, step):
            with eng.Fori(0, BATCH) as b:
                for c in range(CH):
                    step(b, c, b * CH + c)

        @block.sync
        def _(sp):
            for dst, src in loads:
                sp.dma_start(dst, src).then_inc(w_in, 16)

            def step(b, c, n):
                for x, dram in enumerate((parts_q, parts_k)):
                    sp.wait_ge(split[x], n * 4 + 4)
                    for part in range(3):
                        view = dram[part].rearrange("(b f h) d n -> b (h d) f n", b=BATCH, f=HALVES)
                        sp.dma_start(view[bass.ds(b, 1), :, :, c * 512:(c + 1) * 512].rearrange("b p f n -> (b p) f n"),
                                     parts[x][:, part, :, :]).then_inc(stored[x], 16)

            every_chunk(sp, step)
            for x in range(2):
                sp.wait_ge(stored[x], 48 * BATCH * CH)

        @block.vector
        def _(dve):
            if latent:
                nc.vector.memset(ones[:], 1.0).then_inc(ones_set, 1)

            def step(b, c, n):
                dve.wait_ge(turned, n)
                for j in range(CHUNK):
                    t = b * (CH * CHUNK) + (c * CHUNK + j)
                    nc.vector.tensor_scalar(rows[:, j, :], resid[:, bass.ds(t, 1), :].rearrange("p a d -> p (a d)"),
                                            mean[:, bass.ds(t, 1)], rstd[:, bass.ds(t, 1)], ALU.subtract, ALU.mult
                                            ).then_inc(normed, 1)
                for x in range(2):
                    dve.wait_ge(out[x], n + 1)
                    dve.wait_ge(stored[x], n * 48)
                    for k, op in enumerate((
                            lambda: nc.vector.tensor_copy(parts[x][:, 0, :, :], whole[x][:]),
                            lambda: nc.vector.tensor_tensor(rest[x][:], whole[x][:], parts[x][:, 0, :, :], ALU.subtract),
                            lambda: nc.vector.tensor_copy(parts[x][:, 1, :, :], rest[x][:]),
                            lambda: nc.vector.tensor_tensor(parts[x][:, 2, :, :], rest[x][:], parts[x][:, 1, :, :],
                                                            ALU.subtract))):
                        if k:
                            dve.wait_ge(split[x], n * 4 + k)
                        op().then_inc(split[x], 1)

            every_chunk(dve, step)

        @block.tensor
        def _(pe):
            pe.wait_ge(w_in, 16 * len(loads))
            if latent:
                pe.wait_ge(ones_set, 1)

            def step(b, c, n):
                pe.wait_ge(normed, n * CHUNK + CHUNK)
                pe.wait_ge(copied, n)
                for j in range(CHUNK):
                    for f in range(HALVES):
                        m = nc.tensor.transpose(ps_t[:, f, j * 128:(j + 1) * 128], rows[:, j, f * 128:(f + 1) * 128], ident[:])
                m.then_inc(turned, 1)
                pe.wait_ge(copied, n + 1)
                for x in range(2):
                    if x == 1 and latent:
                        pe.wait_ge(v_stored, n)
                        for k in range(HALVES):
                            m = nc.tensor.matmul(ps_v[0:LATENT, 0:2, :].rearrange("p a d -> p (a d)"), wl[:, k, :],
                                                 rows_t[:, k, :], start=k == 0, stop=k == HALVES - 1)
                        m.then_inc(lat_done, 1)
                        pe.wait_ge(lat_copied, n + 1)
                    pe.wait_ge(out[x], n)
                    for f in range(HALVES):
                        wx, src, kn = (wq, rows_t, HALVES) if x == 0 else (wk, rows_t, KN)
                        for k in range(kn):
                            rhs = lat[:] if x == 1 and latent else src[:, k, :]
                            m = nc.tensor.matmul(ps_qk[x][:, f, :], wx[:, k, f * 128:(f + 1) * 128], rhs,
                                                 start=k == 0, stop=k == kn - 1)
                    m.then_inc(done[x], 1)
                pe.wait_ge(v_stored, n)
                for j in range(CHUNK):
                    for k in range(KN):
                        src = lat[:, j * 128:(j + 1) * 128] if latent else rows_t[:, k, j * 128:(j + 1) * 128]
                        m = nc.tensor.matmul(ps_v[:, j, :], src, wv[:, k, :], start=k == 0,
                                             stop=k == KN - 1 and not latent)
                    if latent:
                        m = nc.tensor.matmul(ps_v[:, j, :], ones[:], bias_v[:], start=False, stop=True)
                m.then_inc(v_done, 1)

            every_chunk(pe, step)

        @block.scalar
        def _(act):
            act.wait_ge(w_in, 16 * len(loads))

            def step(b, c, n):
                act.wait_ge(turned, n + 1)
                nc.scalar.copy(rows_t[:], ps_t[:]).then_inc(copied, 1)
                for x in range(2):
                    if x == 1 and latent:
                        act.wait_ge(lat_done, n + 1)
                        nc.scalar.activation(lat[:], ps_v[0:LATENT, 0:2, :].rearrange("p a d -> p (a d)"), ACT.Identity,
                                             bias=bias_l[:]).then_inc(lat_copied, 1)
                    act.wait_ge(done[x], n + 1)
                    act.wait_ge(split[x], n * 4)
                    if latent:
                        for f in range(HALVES):
                            m = nc.scalar.activation(whole[x][:, f, :], ps_qk[x][:, f, :], ACT.Identity,
                                                     bias=bias_qk[:, x, f:f + 1])
                        m.then_inc(out[x], 1)
                    else:
                        nc.scalar.copy(whole[x][:], ps_qk[x][:]).then_inc(out[x], 1)
                act.wait_ge(v_done, n + 1)
                for j in range(CHUNK):
                    m = nc.scalar.copy(values[:, bass.ds(b * HEADS, HEADS), c * CHUNK + j, :],
                                       ps_v[:, j, :].rearrange("p (h d) -> p h d", d=HEAD_DIM))
                m.then_inc(v_stored, 1)

            every_chunk(act, step)


def project_out(nc, resid, attended, ident, w_out, b_out, tag):
    with ExitStack() as ctx:
        sb, pm, sem = alloc(nc, ctx, tag)
        wo = sb("wo", [128, HALVES, DIM], F32)
        bo = sb("bo", [1, DIM], F32)
        ones = sb("ones", [1, 128], F32)
        rows = [sb(f"rows{s}", [128, CHUNK, DIM], F32) for s in range(2)]
        rows_t = [sb(f"rows_t{s}", [128, HALVES, 512], F32) for s in range(2)]
        ps_t = [pm(f"ps_t{s}", [128, HALVES, 512], F32) for s in range(2)]
        ps_y = [pm(f"ps_y{s}", [128, CHUNK, DIM], F32) for s in range(2)]
        w_in, ones_set, staged, turned, copied, done, added = (
            sem(n) for n in ("w_in", "ones_set", "staged", "turned", "copied", "done", "added"))
        CH = TILES // CHUNK // BATCH
        block = ctx.enter_context(nc.Block())

        def every_chunk(eng, step):
            with eng.Fori(0, BATCH) as b:
                for c in range(CH):
                    step(b, c, b * CH + c, c % 2)

        @block.sync
        def _(sp):
            for k in range(HALVES):
                sp.dma_start(wo[:, k, :], w_out[k * 128:(k + 1) * 128, :]).then_inc(w_in, 16)
            sp.dma_start(bo[:], b_out.unsqueeze(0)).then_inc(w_in, 16)

        @block.gpsimd
        def _(pool):
            def step(b, c, n, s):
                pool.wait_ge(turned, n)
                for j in range(CHUNK):
                    m = nc.gpsimd.tensor_copy(rows[s][:, j, :].rearrange("p (h d) -> p h d", d=HEAD_DIM),
                                              attended[:, bass.ds(b * HEADS, HEADS), c * CHUNK + j, :])
                    m.then_inc(staged, 1)

            every_chunk(pool, step)

        @block.tensor
        def _(pe):
            pe.wait_ge(w_in, 16 * (HALVES + 1))
            pe.wait_ge(ones_set, 1)

            def step(b, c, n, s):
                pe.wait_ge(staged, n * CHUNK + CHUNK)
                for j in range(CHUNK):
                    for f in range(HALVES):
                        m = nc.tensor.transpose(ps_t[s][:, f, j * 128:(j + 1) * 128], rows[s][:, j, f * 128:(f + 1) * 128],
                                                ident[:])
                m.then_inc(turned, 1)
                pe.wait_ge(copied, n + 1)
                pe.wait_ge(added, n)
                for j in range(CHUNK):
                    for k in range(HALVES):
                        nc.tensor.matmul(ps_y[s][:, j, :], rows_t[s][:, k, j * 128:(j + 1) * 128], wo[:, k, :],
                                         start=k == 0, stop=False)
                    m = nc.tensor.matmul(ps_y[s][:, j, :], ones[:], bo[:], start=False, stop=True)
                m.then_inc(done, 1)

            every_chunk(pe, step)

        @block.scalar
        def _(act):
            def step(b, c, n, s):
                act.wait_ge(turned, n + 1)
                nc.scalar.copy(rows_t[s][:], ps_t[s][:]).then_inc(copied, 1)

            every_chunk(act, step)

        @block.vector
        def _(dve):
            nc.vector.memset(ones[:], 1.0).then_inc(ones_set, 1)

            def step(b, c, n, s):
                dve.wait_ge(done, n + 1)
                into = resid[:, bass.ds(b * (CH * CHUNK) + c * CHUNK, CHUNK), :]
                nc.vector.tensor_tensor(into, into, ps_y[s][:], ALU.add).then_inc(added, 1)

            every_chunk(dve, step)


def alibi_rows():
    slopes = np.array([1.0 / (256 ** (1.0 / HEADS)) ** (h + 1) for h in range(HEADS)], np.float32)
    rest = (slopes[:, None].astype(np.float64) * np.arange(SEQ)[None, :] / 4)
    bits = np.zeros((2, PAIRS, 6, SEQ), np.uint16)
    one, sign = np.uint16(0x3F80), np.uint16(0x8000)
    bits[0, :, 0:3], bits[1, :, 3:6] = one, one
    for part in range(3):
        top = (rest.astype(np.float32).view(np.uint32) >> 16).astype(np.uint16)
        rest = rest - (top.astype(np.uint32) << 16).view(np.float32)
        for b in range(BATCH):
            bits[0, b * HEADS:(b + 1) * HEADS, 3 + part] = top | sign
            bits[1, b * HEADS:(b + 1) * HEADS, part] = top
    return bits


def attention_layer(nc, resid, ident, w, w_out, b_out, alibi, scale, tag):
    shape = (3, PAIRS, HEAD_DIM, SEQ)
    parts_q = nc.dram_tensor(f"{tag}_parts_q", shape, BF16).ap()
    parts_k = nc.dram_tensor(f"{tag}_parts_k", shape, BF16).ap()
    with ExitStack() as ctx:
        sb, _, _ = alloc(nc, ctx, tag)
        values = sb("values", [128, PAIRS, SEQ // 128, HEAD_DIM], F32)
        attended = sb("attended", [128, PAIRS, SEQ // 128, HEAD_DIM], F32)
        mean, rstd = sb("mean", [128, TILES], F32), sb("rstd", [128, TILES], F32)
        norm_stats(nc, resid, mean, rstd, tag + "n")
        project_qkv(nc, resid, mean, rstd, ident, parts_q, parts_k, values, w, tag + "p")
        rows = None if alibi is None else (alibi[0].bitcast(BF16), alibi[1].bitcast(BF16))
        attention_core(nc, parts_q, parts_k, values, attended, rows, scale, PAIRS, tag + "c")
        project_out(nc, resid, attended, ident, w_out, b_out, tag + "o")


def gate(nc, resid, mean, rstd, ident, gate_w, gate_b, rows_out, logits, tag):
    with ExitStack() as ctx:
        sb, pm, sem = alloc(nc, ctx, tag)
        gw = sb("gw", [128, HALVES, EXPERTS], F32)
        gb = sb("gb", [1, EXPERTS], F32)
        ones = sb("ones", [1, 128], F32)
        rows = [sb(f"rows{s}", [128, CHUNK, DIM], F32) for s in range(2)]
        rows_t = [sb(f"rows_t{s}", [128, HALVES, 512], F32) for s in range(2)]
        ps_t = [pm(f"ps_t{s}", [128, HALVES, 512], F32) for s in range(2)]
        ps_g = [pm(f"ps_g{s}", [128, CHUNK, EXPERTS], F32) for s in range(2)]
        w_in, ones_set, normed, turned, copied, done, kept = (
            sem(n) for n in ("w_in", "ones_set", "normed", "turned", "copied", "done", "kept"))
        rows_stored = [sem(f"rows_stored{s}") for s in range(2)]
        CH = TILES // CHUNK
        block = ctx.enter_context(nc.Block())

        def every_chunk(eng, step):
            with eng.Fori(0, CH // 2) as i:
                for s in range(2):
                    step(i, i * 2 + s, s)

        @block.sync
        def _(sp):
            for k in range(HALVES):
                sp.dma_start(gw[:, k, :], gate_w[k * 128:(k + 1) * 128, :]).then_inc(w_in, 16)
            sp.dma_start(gb[:], gate_b.unsqueeze(0)).then_inc(w_in, 16)
            view = rows_out.rearrange("(t p) d -> p t d", p=128)

            def step(i, n, s):
                sp.wait_ge(normed, n * CHUNK + CHUNK)
                sp.dma_start(view[:, bass.ds(n * CHUNK, CHUNK), :], rows[s][:]).then_inc(rows_stored[s], 16)

            every_chunk(sp, step)
            for s in range(2):
                sp.wait_ge(rows_stored[s], 16 * (CH // 2))

        @block.vector
        def _(dve):
            nc.vector.memset(ones[:], 1.0).then_inc(ones_set, 1)

            def step(i, n, s):
                dve.wait_ge(turned, n)
                dve.wait_ge(rows_stored[s], i * 16)
                for j in range(CHUNK):
                    t = n * CHUNK + j
                    nc.vector.tensor_scalar(rows[s][:, j, :], resid[:, bass.ds(t, 1), :].rearrange("p a d -> p (a d)"),
                                            mean[:, bass.ds(t, 1)], rstd[:, bass.ds(t, 1)], ALU.subtract, ALU.mult
                                            ).then_inc(normed, 1)

            every_chunk(dve, step)

        @block.tensor
        def _(pe):
            pe.wait_ge(w_in, 16 * (HALVES + 1))
            pe.wait_ge(ones_set, 1)

            def step(i, n, s):
                pe.wait_ge(normed, n * CHUNK + CHUNK)
                for j in range(CHUNK):
                    for f in range(HALVES):
                        m = nc.tensor.transpose(ps_t[s][:, f, j * 128:(j + 1) * 128], rows[s][:, j, f * 128:(f + 1) * 128],
                                                ident[:])
                m.then_inc(turned, 1)
                pe.wait_ge(copied, n + 1)
                pe.wait_ge(kept, n)
                for j in range(CHUNK):
                    for k in range(HALVES):
                        nc.tensor.matmul(ps_g[s][:, j, :], rows_t[s][:, k, j * 128:(j + 1) * 128], gw[:, k, :],
                                         start=k == 0, stop=False)
                    m = nc.tensor.matmul(ps_g[s][:, j, :], ones[:], gb[:], start=False, stop=True)
                m.then_inc(done, 1)

            every_chunk(pe, step)

        @block.scalar
        def _(act):
            def step(i, n, s):
                act.wait_ge(turned, n + 1)
                nc.scalar.copy(rows_t[s][:], ps_t[s][:]).then_inc(copied, 1)
                act.wait_ge(done, n + 1)
                nc.scalar.copy(logits[:, bass.ds(n * CHUNK, CHUNK), :], ps_g[s][:]).then_inc(kept, 1)

            every_chunk(act, step)


def route(nc, logits, weight, slots, slot_token, block_rows, tag):
    with ExitStack() as ctx:
        sb, pm, sem = alloc(nc, ctx, tag)
        E3 = [128, TILES, EXPERTS]
        NS = BLOCKS * SUBS
        prob, z, tie, eq, pick1, pick2, chosen = (sb(n, E3, F32) for n in (
            "prob", "z", "tie", "eq", "pick1", "pick2", "chosen"))
        totals, upto, pos, hit = (sb(n, E3, F32) for n in ("totals", "upto", "pos", "hit"))
        top, total, inv, cand = (sb(n, [128, TILES], F32) for n in ("top", "total", "inv", "cand"))
        best = [sb(f"best{k}", [128, TILES], F32) for k in range(2)]
        slot_f = [sb(f"slot_f{k}", [128, TILES], F32) for k in range(2)]
        part_i = sb("part_i", [128, TILES, 2], I32)
        low = sb("low", [128, TILES, 2], F32)
        high = sb("high", [128, TILES, 2], F32)
        ones = sb("ones", [128, 128], F32)
        before = sb("before", [128, 128], F32)
        fill = sb("fill", [128, EXPERTS, TOKENS // BLOCK], F32)
        full = sb("full", [128, EXPERTS, TOKENS // BLOCK], F32)
        blocks, ends, base = (sb(n, [128, EXPERTS], F32) for n in ("blocks", "ends", "base"))
        block_no = sb("block_no", [128, BLOCKS, EXPERTS], F32)
        past = sb("past", [128, BLOCKS, EXPERTS], F32)
        expert = sb("expert", [128, BLOCKS], F32)
        lane = sb("lane", [128, 1], F32)
        column = sb("column", [128, 128], F32)
        token = sb("token", [128, TILES], F32)
        low_hot = [sb(f"low_hot{s}", [128, 128], F32) for s in range(2)]
        high_hot = [sb(f"high_hot{s}", [128, NS], F32) for s in range(2)]
        ps_rank = pm("ps_rank", E3, F32)
        ps_total = pm("ps_total", E3, F32)
        ps_slot = pm("ps_slot", [128, NS], F32)
        consts, chained, exp_done, counted, hot, used, made = (
            sem(n) for n in ("consts", "chained", "exp_done", "counted", "hot", "used", "made"))
        block = ctx.enter_context(nc.Block())
        marks = {}

        @block.gpsimd
        def _(pool):
            io = dict(allow_small_or_imprecise_dtypes=True)
            nc.gpsimd.iota(tie[:], pattern=[[0, TILES], [-1, EXPERTS]], base=EXPERTS, channel_multiplier=0, **io).then_inc(consts, 1)
            nc.gpsimd.iota(fill[:], pattern=[[0, EXPERTS], [BLOCK, TOKENS // BLOCK]], base=0, channel_multiplier=0, **io).then_inc(consts, 1)
            nc.gpsimd.iota(block_no[:], pattern=[[1, BLOCKS], [0, EXPERTS]], base=0, channel_multiplier=0, **io).then_inc(consts, 1)
            nc.gpsimd.iota(lane[:], pattern=[[0, 1]], base=0, channel_multiplier=1, **io).then_inc(consts, 1)
            nc.gpsimd.iota(column[:], pattern=[[1, 128]], base=0, channel_multiplier=0, **io).then_inc(consts, 1)
            nc.gpsimd.iota(token[:], pattern=[[128, TILES]], base=0, channel_multiplier=1, **io).then_inc(consts, 1)

        @block.vector
        def _(dve):
            dve.wait_ge(consts, 6)
            chain = Chain(dve, chained)
            do = chain.step
            v = nc.vector
            wide = lambda x: x[:].unsqueeze(2).to_broadcast(E3)
            do(v.memset(ones[:], 1.0))
            do(v.tensor_scalar(before[:], column[:], lane[:], None, ALU.is_gt))
            do(v.tensor_reduce(top[:], logits[:], AX.X, ALU.max))
            do(v.tensor_tensor(z[:], logits[:], wide(top), ALU.subtract))
            marks["z"] = chain.n
            dve.wait_ge(exp_done, 1)
            do(v.tensor_reduce(total[:], prob[:], AX.X, ALU.add))
            do(v.reciprocal(inv[:], total[:]))
            do(v.tensor_tensor(prob[:], prob[:], wide(inv), ALU.mult))
            for k, pick in enumerate((pick1, pick2)):
                do(v.tensor_reduce(best[k][:], prob[:], AX.X, ALU.max))
                do(v.tensor_tensor(eq[:], prob[:], wide(best[k]), ALU.is_equal))
                do(v.tensor_tensor(eq[:], eq[:], tie[:], ALU.mult))
                do(v.tensor_reduce(cand[:], eq[:], AX.X, ALU.max))
                do(v.tensor_tensor(pick[:], eq[:], wide(cand), ALU.is_equal))
                if k == 0:
                    do(v.scalar_tensor_tensor(prob[:], pick[:], -4.0, prob[:], ALU.mult, ALU.add))
            do(v.tensor_tensor(chosen[:], pick1[:], pick2[:], ALU.add))
            marks["chosen"] = chain.n
            do(v.tensor_tensor(total[:], best[0][:], best[1][:], ALU.add))
            do(v.tensor_scalar(total[:], total[:], 1e-20, None, ALU.add))
            do(v.reciprocal(inv[:], total[:]))
            for k in range(2):
                do(v.tensor_tensor(weight[:, :, k], best[k][:], inv[:], ALU.mult))
            dve.wait_ge(counted, 1)
            do(v.tensor_copy(totals[:], ps_total[:]))
            for e in range(EXPERTS):
                do(v.tensor_tensor_scan(upto[:, :, e], ones[:, 0:TILES], totals[:, :, e], 0.0, ALU.mult, ALU.add))
            count = upto[:, TILES - 1, :].unsqueeze(2).to_broadcast([128, EXPERTS, TOKENS // BLOCK])
            do(v.tensor_tensor(full[:], count, fill[:], ALU.is_gt))
            do(v.tensor_reduce(blocks[:], full[:], AX.X, ALU.add))
            do(v.tensor_tensor_scan(ends[:], ones[:, 0:EXPERTS], blocks[:], 0.0, ALU.mult, ALU.add))
            do(v.tensor_tensor(base[:], ends[:], blocks[:], ALU.subtract))
            do(v.tensor_scalar(base[:], base[:], float(BLOCK), None, ALU.mult))
            do(v.tensor_tensor(pos[:], upto[:], totals[:], ALU.subtract))
            do(v.tensor_tensor(pos[:], pos[:], ps_rank[:], ALU.add))
            do(v.tensor_tensor(pos[:], pos[:], base[:].unsqueeze(1).to_broadcast(E3), ALU.add))
            for k, pick in enumerate((pick1, pick2)):
                do(v.tensor_tensor(hit[:], pick[:], pos[:], ALU.mult))
                do(v.tensor_reduce(slot_f[k][:], hit[:], AX.X, ALU.add))
                do(v.tensor_copy(slots[:, :, k], slot_f[k][:]))
            do(v.tensor_tensor(past[:], block_no[:], ends[:].unsqueeze(1).to_broadcast([128, BLOCKS, EXPERTS]), ALU.is_ge))
            do(v.tensor_reduce(expert[:], past[:], AX.X, ALU.add))
            do(v.tensor_scalar(expert[:], expert[:], float(EXPERTS - 1), 128.0, ALU.min, ALU.mult))
            do(v.tensor_scalar(block_rows[:], expert[:], lane[:], None, ALU.add))
            do(v.tensor_scalar(part_i[:], slots[:], 7, None, ALU.logical_shift_right))
            do(v.tensor_copy(high[:], part_i[:]))
            do(v.tensor_scalar(part_i[:], slots[:], 127, None, ALU.bitwise_and))
            do(v.tensor_copy(low[:], part_i[:]))
            with dve.Fori(0, TILES) as t:
                for k in range(2):
                    dve.wait_ge(used, t * 2 + k)
                    v.tensor_scalar(low_hot[k][:], column[:], low[:, bass.ds(t, 1), k], token[:, bass.ds(t, 1)],
                                    ALU.is_equal, ALU.mult).then_inc(hot, 1)
                    v.tensor_scalar(high_hot[k][:], column[:, 0:NS], high[:, bass.ds(t, 1), k], None,
                                    ALU.is_equal).then_inc(hot, 1)
            dve.wait_ge(used, 2 * TILES)
            do(v.tensor_copy(slot_token[:], ps_slot[:]))

        @block.scalar
        def _(act):
            act.wait_ge(chained, marks["z"])
            nc.scalar.activation(prob[:], z[:], ACT.Exp).then_inc(exp_done, 1)

        @block.tensor
        def _(pe):
            pe.wait_ge(chained, marks["chosen"])
            nc.tensor.matmul(ps_rank[:], before[:], chosen[:], start=True, stop=True)
            nc.tensor.matmul(ps_total[:], ones[:], chosen[:], start=True, stop=True).then_inc(counted, 1)

            def add(t, k, first, last):
                pe.wait_ge(hot, t * 4 + 2 * k + 2)
                nc.tensor.matmul(ps_slot[:], low_hot[k][:], high_hot[k][:], start=first, stop=last).then_inc(used, 1)

            add(0, 0, True, False)
            add(0, 1, False, False)
            with pe.Fori(1, TILES - 1) as t:
                for k in range(2):
                    add(t, k, False, False)
            add(TILES - 1, 0, False, False)
            add(TILES - 1, 1, False, True)


class Turn:

    def __init__(self, of, turn, c):
        self.of, self.turn, self.c = of, turn, c
        self.n = turn * of + c
        self.slot = c % of
        self.fills = turn + (c // of + 1)
        self.first = isinstance(turn, int) and c == 0

    def ahead(self, k):
        return Turn(self.of, self.turn, self.c + k)


def experts(nc, rows_in, table, slot_token, block_rows, slot_out, ident, tag):
    with ExitStack() as ctx:
        sb, pm, sem = alloc(nc, ctx, tag)
        R = 3
        which = [sb(f"which{s}", [128, SUBS + 1], I32) for s in range(R)]
        wts = [sb(f"wts{s}", [128, EROW], F32) for s in range(R)]
        rows = [sb(f"rows{s}", [128, SUBS, DIM], F32) for s in range(R)]
        rows_t = [sb(f"rows_t{s}", [128, HALVES, BLOCK], F32) for s in range(R)]
        gated = [sb(f"gated{s}", [128, BLOCK], F32) for s in range(R)]
        prod = [sb(f"prod{s}", [128, BLOCK], F32) for s in range(R)]
        hid = [sb(f"hid{s}", [128, FT, BLOCK], F32) for s in range(R)]
        outs = [sb(f"outs{s}", [128, SUBS, DIM], F32) for s in range(R)]
        ps_t = pm("ps_t", [128, HALVES, BLOCK], F32)
        ps_h = [pm(f"ps_h{s}", [128, 2, BLOCK], F32) for s in range(R)]
        ps_y = [pm(f"ps_y{s}", [128, SUBS, DIM], F32) for s in range(R)]
        ones_set = sem("ones_set")
        turned = sem("turned")
        copied = sem("copied")
        scored = sem("scored")
        gate_out = sem("gate_out")
        prod_out = sem("prod_out")
        hid_out = sem("hid_out")
        down_done = sem("down_done")
        outs_out = sem("outs_out")
        w_in = [sem(f"w_in{s}", lasting=True) for s in range(R)]
        x_in = [sem(f"x_in{s}", lasting=True) for s in range(R)]
        y_out = [sem(f"y_out{s}") for s in range(R)]
        block = ctx.enter_context(nc.Block())
        PARTS = [(m, 128 if m < FT - 1 else FREST) for m in range(FT)]
        DOWN_AT = 2
        assert BLOCKS % R == 0

        def bank(b, m):
            return (b.c * FT + m) % R

        def every_block(eng, step):
            step(Turn(R, 0, 0), False)
            with eng.Fori(0, BLOCKS // R - 1) as i:
                for c in range(1, R + 1):
                    step(Turn(R, i, c), False)
            for c in range(BLOCKS - R + 1, BLOCKS):
                step(Turn(R, 0, c), c == BLOCKS - 1)

        @block.gpsimd
        def _(pool):
            def step(b, last):
                pool.wait_ge(down_done, b.n + 1)
                s = b.slot
                nc.gpsimd.tensor_copy(which[s][:, 0:1], block_rows[:, bass.ds(b.n, 1)])
                nc.gpsimd.tensor_copy(which[s][:, 1:1 + SUBS], slot_token[:, bass.ds(b.n * SUBS, SUBS)])
                pool.drain()
                for j in range(SUBS):
                    nc.gpsimd.indirect_dma_start(rows[s][:, j, :], None, rows_in, bass.IndirectOffsetOnAxis(
                        ap=which[s][:, 1 + j:2 + j], axis=0)).then_inc(x_in[s], 16)
                nc.gpsimd.indirect_dma_start(wts[s][:], None, table, bass.IndirectOffsetOnAxis(
                    ap=which[s][:, 0:1], axis=0)).then_inc(w_in[s], 16)

            every_block(pool, step)

        @block.tensor
        def _(pe):
            nc.tensor.nop().then_inc(down_done, R)

            def turn_rows(b):
                pe.wait_ge(x_in[b.slot], b.fills * 16 * SUBS)
                pe.wait_ge(copied, b.n + 1)
                for j in range(SUBS):
                    for f in range(HALVES):
                        mm = nc.tensor.transpose(ps_t[:, f, j * 128:(j + 1) * 128],
                                                 rows[b.slot][:, j, f * 128:(f + 1) * 128], ident[:])
                mm.then_inc(turned, 1)

            def down(b):
                pe.wait_ge(hid_out, (b.n + 1) * FT + R)
                pe.wait_ge(outs_out, b.n + 1)
                for j in range(SUBS):
                    for m, size in PARTS:
                        k = size if m < FT - 1 else size + 1
                        mm = nc.tensor.matmul(ps_y[b.slot][:, j, :], hid[b.slot][0:k, m, j * 128:(j + 1) * 128],
                                              wts[b.slot][0:k, DOWN + m * DIM:DOWN + (m + 1) * DIM],
                                              start=m == 0, stop=m == FT - 1)
                mm.then_inc(down_done, 1)

            def step(b, last):
                s = b.slot
                pe.wait_ge(w_in[s], b.fills * 16)
                pe.wait_ge(copied, b.n + 2)
                for m, size in PARTS:
                    if m == DOWN_AT:
                        if not b.first:
                            down(b.ahead(-1))
                        if not last:
                            turn_rows(b.ahead(1))
                    pe.wait_ge(prod_out, b.n * FT + m + 1)
                    for x, at in ((0, UP), (1, GATE)):
                        for k in range(HALVES):
                            c = at + k * FFN + m * 128
                            mm = nc.tensor.matmul(ps_h[bank(b, m)][0:size, x, :], wts[s][:, c:c + size],
                                                  rows_t[s][:, k, :], start=k == 0, stop=k == HALVES - 1)
                    mm.then_inc(scored, 1)

            turn_rows(Turn(R, 0, 0))
            every_block(pe, step)
            down(Turn(R, 0, BLOCKS - 1))

        @block.scalar
        def _(act):
            nc.scalar.nop().then_inc(copied, 1)
            nc.scalar.nop().then_inc(hid_out, R)
            act.wait_ge(ones_set, R)

            def copy_rows(b):
                act.wait_ge(turned, b.n + 1)
                nc.scalar.copy(rows_t[b.slot][:], ps_t[:]).then_inc(copied, 1)

            def silu(b, m):
                size = PARTS[m][1]
                act.wait_ge(prod_out, b.n * FT + m + 1 + R)
                if m == 0:
                    act.wait_ge(down_done, b.n + 1)
                nc.scalar.activation(hid[b.slot][0:size, m, :], prod[bank(b, m)][0:size, :], ACT.Silu).then_inc(hid_out, 1)

            def step(b, last):
                act.wait_ge(w_in[b.slot], b.fills * 16)
                for m, size in PARTS:
                    if m == DOWN_AT and not last:
                        copy_rows(b.ahead(1))
                    act.wait_ge(scored, b.n * FT + m + 1)
                    act.wait_ge(prod_out, b.n * FT + m + 1)
                    nc.scalar.activation(gated[bank(b, m)][0:size, :], ps_h[bank(b, m)][0:size, 1, :], ACT.Identity,
                                         bias=wts[b.slot][0:size, GATEB + m:GATEB + m + 1]).then_inc(gate_out, 1)
                    if m:
                        silu(b, m - 1)
                silu(b, FT - 1)

            copy_rows(Turn(R, 0, 0))
            every_block(act, step)

        @block.vector
        def _(dve):
            for s in range(R):
                nc.vector.memset(hid[s][0:64, FT - 1, :], 1.0).then_inc(ones_set, 1)
            nc.vector.nop().then_inc(prod_out, R)
            nc.vector.nop().then_inc(outs_out, R)

            def finish(b):
                dve.wait_ge(down_done, b.n + 1 + R)
                dve.wait_ge(y_out[b.slot], b.fills * 16)
                nc.vector.tensor_copy(outs[b.slot][:], ps_y[b.slot][:]).then_inc(outs_out, 1)

            def step(b, last):
                dve.wait_ge(w_in[b.slot], b.fills * 16)
                for m, size in PARTS:
                    if m == DOWN_AT + 1 and (not b.first):
                        finish(b.ahead(-1))
                    dve.wait_ge(gate_out, b.n * FT + m + 1)
                    dve.wait_ge(hid_out, b.n * FT + m + 1)
                    nc.vector.scalar_tensor_tensor(prod[bank(b, m)][0:size, :], ps_h[bank(b, m)][0:size, 0, :],
                                                   wts[b.slot][0:size, UPB + m:UPB + m + 1], gated[bank(b, m)][0:size, :],
                                                   ALU.add, ALU.mult).then_inc(prod_out, 1)

            every_block(dve, step)
            finish(Turn(R, 0, BLOCKS - 1))

        @block.sync
        def _(sp):
            for s in range(R):
                nc.sync.nop().then_inc(y_out[s], 16)
            view = slot_out.rearrange("(n j p) d -> p n j d", p=128, j=SUBS)

            def step(b, last):
                sp.wait_ge(outs_out, b.n + 1 + R)
                sp.dma_start(view[:, bass.ds(b.n, 1), :, :].rearrange("p a j d -> p (a j) d"), outs[b.slot][:]
                             ).then_inc(y_out[b.slot], 16)

            every_block(sp, step)
            for s in range(R):
                sp.wait_ge(y_out[s], 16 * (BLOCKS // R) + 16)


def combine(nc, resid, slots, weight, slot_out, tag):
    with ExitStack() as ctx:
        sb, _, sem = alloc(nc, ctx, tag)
        N = 4
        which = [sb(f"which{s}", [128, 2], I32) for s in range(N)]
        got = [sb(f"got{s}", [128, 2, DIM], F32) for s in range(N)]
        gathered = [sem(f"gathered{s}", lasting=True) for s in range(N)]
        added = sem("added")
        block = ctx.enter_context(nc.Block())

        @block.gpsimd
        def _(pool):
            with pool.Fori(0, TILES // N) as i:
                for s in range(N):
                    pool.wait_ge(added, i * (2 * N) + 2 * s + 2)
                    nc.gpsimd.tensor_copy(which[s][:], slots[:, bass.ds(i * N + s, 1), :].rearrange("p a k -> p (a k)"))
                    pool.drain()
                    for k in range(2):
                        nc.gpsimd.indirect_dma_start(got[s][:, k, :], None, slot_out, bass.IndirectOffsetOnAxis(
                            ap=which[s][:, k:k + 1], axis=0)).then_inc(gathered[s], 16)

        @block.vector
        def _(dve):
            nc.vector.nop().then_inc(added, 2 * N)
            with dve.Fori(0, TILES // N) as i:
                for s in range(N):
                    t = i * N + s
                    dve.wait_ge(gathered[s], i * 32 + 32)
                    row = resid[:, bass.ds(t, 1), :].rearrange("p a d -> p (a d)")
                    for k in range(2):
                        if k:
                            dve.wait_ge(added, t * 2 + 1 + 2 * N)
                        nc.vector.scalar_tensor_tensor(row, got[s][:, k, :], weight[:, bass.ds(t, 1), k], row,
                                                       ALU.mult, ALU.add).then_inc(added, 1)


def moe_layer(nc, resid, ident, a, tag):
    rows = nc.dram_tensor(f"{tag}_rows", (TOKENS, DIM), F32).ap()
    slot_out = nc.dram_tensor(f"{tag}_slot_out", (BLOCKS * BLOCK, DIM), F32).ap()
    with ExitStack() as ctx:
        sb, _, _ = alloc(nc, ctx, tag)
        mean, rstd = sb("mean", [128, TILES], F32), sb("rstd", [128, TILES], F32)
        logits = sb("logits", [128, TILES, EXPERTS], F32)
        weight = sb("weight", [128, TILES, 2], F32)
        slots = sb("slots", [128, TILES, 2], I32)
        slot_token = sb("slot_token", [128, BLOCKS * SUBS], I32)
        block_rows = sb("block_rows", [128, BLOCKS], I32)
        norm_stats(nc, resid, mean, rstd, tag + "n")
        gate(nc, resid, mean, rstd, ident, a["gate_w"], a["gate_b"], rows, logits, tag + "g")
        route(nc, logits, weight, slots, slot_token, block_rows, tag + "r")
        experts(nc, rows, a["experts"], slot_token, block_rows, slot_out, ident, tag + "e")
        combine(nc, resid, slots, weight, slot_out, tag + "c")


def moe_arrays(z):
    C = np.ascontiguousarray
    g = lambda k: np.asarray(z["L0_ffn_" + k])
    out = np.zeros((EXPERTS, 128, EROW), np.float32)
    for at, name in ((UP, "up"), (GATE, "gp")):
        w = g(name + "_w").reshape(EXPERTS, FFN, HALVES, 128).transpose(0, 3, 2, 1)
        out[:, :, at:at + HALVES * FFN] = w.reshape(EXPERTS, 128, HALVES * FFN)
    down = g("down_w").transpose(0, 2, 1)
    for m in range(FT):
        size = 128 if m < FT - 1 else FREST
        out[:, 0:size, DOWN + m * DIM:DOWN + (m + 1) * DIM] = down[:, m * 128:m * 128 + size]
        for at, name in ((UPB, "up_b"), (GATEB, "gp_b")):
            out[:, 0:size, at + m] = g(name)[:, m * 128:m * 128 + size]
    out[:, FREST, DOWN + (FT - 1) * DIM:DOWN + FT * DIM] = g("down_b")
    return {"experts": out.reshape(EXPERTS * 128, EROW), "gate_w": C(g("gate_w").T), "gate_b": C(g("gate_b"))}


MAGIC = 1.5 * 2.0 ** 23
DOWNWARDS = 1.0 - 2.0 ** -23


class Fp4:

    STEPS = 14

    def __init__(self, nc, sb, name, n):
        blocks = n // QUANT
        self.nc, self.n = nc, n
        self.peak, self.scale, self.inv = (sb(f"{name}_{k}", [128, blocks], F32) for k in ("peak", "scale", "inv"))
        self.a, self.b, self.c = (sb(f"{name}_{k}", [128, n], F32) for k in "abc")

    def run(self, eng, sem, base, x, out, last=None):
        v, n = self.nc.vector, self.n
        wide = lambda s: s[:].unsqueeze(2).to_broadcast([128, n // QUANT, QUANT])
        grouped = lambda t: t.rearrange("p (g q) -> p g q", q=QUANT)
        a, b, c = self.a[:], self.b[:], self.c[:]
        I = lambda t: t.bitcast(I32)
        ops = (
            lambda: v.tensor_reduce(self.peak[:], grouped(x), AX.X, ALU.max, apply_absolute_value=True),
            lambda: v.tensor_scalar(self.scale[:], self.peak[:], 1.0 / 6.0, 1e-12, ALU.mult, ALU.max),
            lambda: v.reciprocal(self.inv[:], self.scale[:]),
            lambda: v.tensor_scalar(self.inv[:], self.inv[:], DOWNWARDS, None, ALU.mult),
            lambda: v.tensor_tensor(grouped(a), grouped(x), wide(self.inv), ALU.mult),
            lambda: v.tensor_scalar(I(a), I(a), 0x7FFFFFFF, None, ALU.bitwise_and),
            lambda: v.tensor_scalar(b, a, 2.0, 4.0, ALU.max, ALU.min),
            lambda: v.tensor_scalar(b, b, MAGIC, MAGIC + 6.0, ALU.add, ALU.subtract),
            lambda: v.tensor_scalar(c, a, 2.0, MAGIC / 2, ALU.min, ALU.add),
            lambda: v.scalar_tensor_tensor(b, c, -MAGIC / 2, b, ALU.add, ALU.add),
            lambda: v.tensor_scalar(c, a, 4.0, MAGIC * 2, ALU.max, ALU.add),
            lambda: v.scalar_tensor_tensor(b, c, -MAGIC * 2, b, ALU.add, ALU.add),
            lambda: v.tensor_tensor(grouped(b), grouped(b), wide(self.scale), ALU.mult),
            lambda: v.scalar_tensor_tensor(I(out), I(x), -0x80000000, I(b), ALU.bitwise_and, ALU.bitwise_or),
        )
        assert len(ops) == self.STEPS
        for k, op in enumerate(ops):
            if k:
                eng.wait_ge(sem, base + k)
            op().then_inc(sem, 1)


def quantise_weights(nc, ident, w_up, w_gate, w_down, up_t, gate_t, down_t, tag):
    with ExitStack() as ctx:
        sb, pm, sem = alloc(nc, ctx, tag)
        quant = {n: Fp4(nc, sb, f"q{n}", n) for n in (DIM, INNER)}
        jobs = []
        for w, dst in ((w_up, up_t), (w_gate, gate_t)):
            for m in range(IT):
                jobs.append((w, dst, m, 128 if m < IT - 1 else IREST, DIM))
        for m in range(HALVES):
            jobs.append((w_down, down_t, m, 128, INNER))
        rows = [sb(f"rows{s}", [128, INNER], F32) for s in range(2)]
        ps = [pm(f"ps{s}", [128, 8, 128], F32) for s in range(2)]
        filled = sem("filled")
        row_in = [sem(f"row_in{s}") for s in range(2)]
        steps, turned, copied = sem("steps"), sem("turned"), sem("copied")
        block = ctx.enter_context(nc.Block())

        @block.sync
        def _(sp):
            sp.wait_ge(filled, 2)
            for n, (w, dst, m, size, width) in enumerate(jobs):
                if n >= 2:
                    sp.wait_ge(turned, n - 1)
                sp.dma_start(rows[n % 2][0:size, 0:width], w[m * 128:m * 128 + size, :]).then_inc(row_in[n % 2], 16)

        @block.vector
        def _(dve):
            for s in range(2):
                nc.vector.memset(rows[s][:], 0.0).then_inc(filled, 1)
            for n, (w, dst, m, size, width) in enumerate(jobs):
                dve.wait_ge(row_in[n % 2], 16 * (n // 2 + 1))
                if n:
                    dve.wait_ge(steps, n * Fp4.STEPS)
                x = rows[n % 2][:, 0:width]
                quant[width].run(dve, steps, n * Fp4.STEPS, x, x)

        @block.tensor
        def _(pe):
            for n, (w, dst, m, size, width) in enumerate(jobs):
                pe.wait_ge(steps, (n + 1) * Fp4.STEPS)
                if n >= 2:
                    pe.wait_ge(copied, n - 1)
                for k in range(-(-width // 128)):
                    c = min(128, width - k * 128)
                    t = nc.tensor.transpose(ps[n % 2][0:c, k, 0:size], rows[n % 2][0:size, k * 128:k * 128 + c],
                                            ident[0:size, 0:size])
                t.then_inc(turned, 1)

        @block.scalar
        def _(act):
            for n, (w, dst, m, size, width) in enumerate(jobs):
                act.wait_ge(turned, n + 1)
                full = width // 128
                c = nc.scalar.copy(dst[:, 0:full, m * 128:m * 128 + size], ps[n % 2][:, 0:full, 0:size])
                if width % 128:
                    c = nc.scalar.copy(dst[0:width % 128, full, m * 128:m * 128 + size],
                                       ps[n % 2][0:width % 128, full, 0:size])
                c.then_inc(copied, 1)


def fp4_mlp(nc, resid, mean, rstd, ident, up_t, gate_t, down_t, out, tag):
    with ExitStack() as ctx:
        sb, pm, sem = alloc(nc, ctx, tag)
        HW = INNER // 2
        qx = Fp4(nc, sb, "qx", DIM)
        qh = Fp4(nc, sb, "qh", INNER)
        rows = [sb(f"rows{s}", [128, DIM], F32) for s in range(2)]
        rows_t = [sb(f"rows_t{s}", [128, HALVES, 128], F32) for s in range(2)]
        act_g = [sb(f"act_g{s}", [128, 2, HW], F32) for s in range(2)]
        hid = [sb(f"hid{s}", [128, INNER], F32) for s in range(2)]
        hid_t = [sb(f"hid_t{s}", [128, IT, 128], F32) for s in range(2)]
        done = [sb(f"done{s}", [128, DIM], F32) for s in range(2)]
        ps_t = pm("ps_t", [128, 8, 128], F32)
        ps_g = pm("ps_g", [128, 2, 512], F32)
        ps_u = pm("ps_u", [128, 2, 512], F32)
        ps_y = pm("ps_y", [128, DIM], F32)
        ps_x = pm("ps_x", [128, HALVES, 128], F32)
        xsteps, hsteps = sem("xsteps"), sem("hsteps")
        xturned, xcopied, scored, silu_done, multiplied, hturned, hcopied, projected, summed = (
            sem(n) for n in ("xturned", "xcopied", "scored", "silu_done", "multiplied", "hturned", "hcopied",
                             "projected", "summed"))
        stored = [sem(f"stored{s}") for s in range(2)]
        XS, HS = Fp4.STEPS + 1, Fp4.STEPS
        block = ctx.enter_context(nc.Block())

        def every_tile(eng, step):
            with eng.Fori(0, TILES // 2) as i:
                for s in range(2):
                    step(i, i * 2 + s, s)

        @block.vector
        def _(dve):
            def norm(i, t, s):
                dve.wait_ge(xturned, t)
                dve.wait_ge(xsteps, t * XS)
                nc.vector.tensor_scalar(rows[s][:], resid[:, bass.ds(t, 1), :].rearrange("p a d -> p (a d)"),
                                        mean[:, bass.ds(t, 1)], rstd[:, bass.ds(t, 1)], ALU.subtract, ALU.mult
                                        ).then_inc(xsteps, 1)
                dve.wait_ge(xsteps, t * XS + 1)
                qx.run(dve, xsteps, t * XS + 1, rows[s][:], rows[s][:])

            def hidden(i, t, s):
                dve.wait_ge(silu_done, t + 1)
                dve.wait_ge(hturned, t)
                dve.wait_ge(hsteps, t * HS)
                nc.vector.tensor_tensor(hid[s][:].rearrange("p (b c) -> p b c", b=2), ps_u[:, :, 0:HW], act_g[s][:], ALU.mult
                                        ).then_inc(multiplied, 1)
                dve.wait_ge(multiplied, t + 1)
                qh.run(dve, hsteps, t * HS, hid[s][:], hid[s][:])

            def finish(i, t, s):
                dve.wait_ge(projected, t + 1)
                dve.wait_ge(stored[s], i * 16)
                nc.vector.tensor_tensor(done[s][:], ps_y[:], resid[:, bass.ds(t, 1), :].rearrange("p a d -> p (a d)"),
                                        ALU.add).then_inc(summed, 1)

            def step(i, t, s, after=True):
                if after:
                    norm(i + s, t + 1, 1 - s)
                hidden(i, t, s)
                finish(i, t, s)

            norm(0, 0, 0)
            with dve.Fori(0, TILES // 2 - 1) as i:
                for s in range(2):
                    step(i, i * 2 + s, s)
            last = TILES // 2 - 1
            step(last, TILES - 2, 0)
            step(last, TILES - 1, 1, False)

        @block.tensor
        def _(pe):
            def turn_x(i, t, s):
                pe.wait_ge(xsteps, t * XS + XS)
                pe.wait_ge(xcopied, t)
                for f in range(HALVES):
                    m = nc.tensor.transpose(ps_x[:, f, :], rows[s][:, f * 128:(f + 1) * 128], ident[:])
                m.then_inc(xturned, 1)

            def score(i, t, s):
                pe.wait_ge(xcopied, t + 1)
                pe.wait_ge(multiplied, t)
                for ps, w in ((ps_g, gate_t), (ps_u, up_t)):
                    for h in range(2):
                        for k in range(HALVES):
                            m = nc.tensor.matmul(ps[:, h, 0:HW], rows_t[s][:, k, :], w[:, k, h * HW:(h + 1) * HW],
                                                 start=k == 0, stop=k == HALVES - 1)
                m.then_inc(scored, 1)

            def down(i, t, s):
                pe.wait_ge(hsteps, t * HS + HS)
                pe.wait_ge(hcopied, t)
                for k in range(IT):
                    c = 128 if k < IT - 1 else IREST
                    m = nc.tensor.transpose(ps_t[0:c, k, :], hid[s][:, k * 128:k * 128 + c], ident[:])
                m.then_inc(hturned, 1)
                pe.wait_ge(hcopied, t + 1)
                pe.wait_ge(summed, t)
                for k in range(IT):
                    c = 128 if k < IT - 1 else IREST
                    m = nc.tensor.matmul(ps_y[:], hid_t[s][0:c, k, :], down_t[0:c, k, :], start=k == 0, stop=k == IT - 1)
                m.then_inc(projected, 1)

            def step(i, t, s, after=True):
                if after:
                    turn_x(i + s, t + 1, 1 - s)
                down(i, t, s)
                if after:
                    score(i + s, t + 1, 1 - s)

            turn_x(0, 0, 0)
            score(0, 0, 0)
            with pe.Fori(0, TILES // 2 - 1) as i:
                for s in range(2):
                    step(i, i * 2 + s, s)
            last = TILES // 2 - 1
            step(last, TILES - 2, 0)
            step(last, TILES - 1, 1, False)

        @block.scalar
        def _(act):
            def copy_x(i, t, s):
                act.wait_ge(xturned, t + 1)
                nc.scalar.copy(rows_t[s][:], ps_x[:]).then_inc(xcopied, 1)

            def silu(i, t, s):
                act.wait_ge(scored, t + 1)
                nc.scalar.activation(act_g[s][:], ps_g[:, :, 0:HW], ACT.Silu).then_inc(silu_done, 1)

            def copy_h(i, t, s):
                act.wait_ge(hturned, t + 1)
                nc.scalar.copy(hid_t[s][:, 0:IT - 1, :], ps_t[:, 0:IT - 1, :])
                nc.scalar.copy(hid_t[s][0:IREST, IT - 1, :], ps_t[0:IREST, IT - 1, :]).then_inc(hcopied, 1)

            def step(i, t, s, after=True):
                if after:
                    copy_x(i + s, t + 1, 1 - s)
                copy_h(i, t, s)
                if after:
                    silu(i + s, t + 1, 1 - s)

            copy_x(0, 0, 0)
            silu(0, 0, 0)
            with act.Fori(0, TILES // 2 - 1) as i:
                for s in range(2):
                    step(i, i * 2 + s, s)
            last = TILES // 2 - 1
            step(last, TILES - 2, 0)
            step(last, TILES - 1, 1, False)

        @block.sync
        def _(sp):
            view = out.rearrange("(t p) d -> p t d", p=128)

            def step(i, t, s):
                sp.wait_ge(summed, t + 1)
                sp.dma_start(view[:, bass.ds(t, 1), :].rearrange("p a d -> p (a d)"), done[s][:]).then_inc(stored[s], 16)

            every_tile(sp, step)
            for s in range(2):
                sp.wait_ge(stored[s], 16 * (TILES // 2))


def ffn_layer(nc, resid, ident, a, out, tag):
    with ExitStack() as ctx:
        sb, _, _ = alloc(nc, ctx, tag)
        mean, rstd = sb("mean", [128, TILES], F32), sb("rstd", [128, TILES], F32)
        up_t = sb("up_t", [128, HALVES, INNER], F32)
        gate_t = sb("gate_t", [128, HALVES, INNER], F32)
        down_t = sb("down_t", [128, IT, DIM], F32)
        norm_stats(nc, resid, mean, rstd, tag + "n")
        quantise_weights(nc, ident, a["w_up"], a["w_gate"], a["w_down"], up_t, gate_t, down_t, tag + "q")
        fp4_mlp(nc, resid, mean, rstd, ident, up_t, gate_t, down_t, out, tag + "m")


def tower(nc, a, out):
    with ExitStack() as ctx:
        resid = ctx.enter_context(nc.sbuf_tensor("resid", [128, TILES, DIM], F32))
        ident = ctx.enter_context(nc.sbuf_tensor("ident", [128, 128], F32))
        make_identity(nc, ident, "id")
        embed(nc, a["ids"], [a["emb0"], a["emb1"], a["emb2"]], [a["w0"], a["w1"], a["w2"]],
              [a["b0"], a["b1"], a["b2"]], resid, ident, "e")
        attention_layer(nc, resid, ident, {k: a["a0_" + k] for k in ("q", "k", "v", "latent", "bq", "bk", "bl", "bv")},
                        a["a0_out"], a["a0_bo"], None, float(HEAD_DIM) ** -0.5, "A")
        moe_layer(nc, resid, ident, a, "M")
        attention_layer(nc, resid, ident, {k: a["a1_" + k] for k in ("q", "k", "v")},
                        a["a1_out"], a["a1_bo"], a["alibi"], float(HEAD_DIM) ** 0.5, "B")
        ffn_layer(nc, resid, ident, a, out, "F")


def kernel(**inputs):
    import concourse.bacc as bacc
    from concourse.bass_utils import run_bass_kernel_spmd

    z = {k: np.asarray(v) for k, v in inputs.items()}
    C = np.ascontiguousarray
    arrays = {"ids": C(z["x"].reshape(TILES, 128).T)}
    for k in range(3):
        arrays[f"emb{k}"] = C(z[f"L0_tok_emb{k}"])
        arrays[f"w{k}"] = C(z[f"L0_tok_w{k}"].T)
        arrays[f"b{k}"] = C(z[f"L0_tok_b{k}"].reshape(1, DIM))
    for name, key in (("q", "Wq"), ("k", "Wk"), ("v", "Wv"), ("latent", "Wl"), ("bl", "bl"), ("bv", "bv"),
                      ("out", "Wo"), ("bo", "bo")):
        arrays["a0_" + name] = C(z["L0_attn_" + key])
    for name in ("bq", "bk"):
        arrays["a0_" + name] = C(z["L0_attn_" + name].reshape(HALVES, 128))
    for name, key in (("q", "Wq"), ("k", "Wk"), ("v", "Wv"), ("out", "Wp")):
        arrays["a1_" + name] = C(z["L1_attn_" + key].T)
    arrays["a1_bo"] = C(z["L1_attn_bp"])
    arrays["alibi"] = alibi_rows()
    arrays.update(moe_arrays(z))
    for name in ("w_gate", "w_up", "w_down"):
        arrays[name] = C(z["L1_ffn_" + name])

    nc = bacc.Bacc("TRN2", target_bir_lowering=False, num_devices=1)
    nc.disable_value_cache = True
    a = {k: nc.dram_tensor(f"in_{k}", v.shape, mybir.dt.from_np(v.dtype), kind="ExternalInput").ap()
         for k, v in arrays.items()}
    out = nc.dram_tensor("out", (TOKENS, DIM), F32, kind="ExternalOutput").ap()
    tower(nc, a, out)
    result = run_bass_kernel_spmd(nc, [{f"in_{k}": v for k, v in arrays.items()}], core_ids=[0])
    return result.results[0]["out"].reshape(BATCH, SEQ, DIM)
```
